# Optimizing a Trainium2 kernel written in Bass

```python
import numpy as np
import jax
import jax.numpy as jnp

def _softmax(x, axis=-1):
    return jax.nn.softmax(x, axis=axis)

def _gelu(x):
    return jax.nn.gelu(x, approximate=True)

def _silu(x):
    return jax.nn.silu(x)

def _sigmoid(x):
    return jax.nn.sigmoid(x)

def _layernorm(x, axis=-1, eps=1e-05):
    m = jnp.mean(x, axis=axis, keepdims=True)
    v = jnp.var(x, axis=axis, keepdims=True)
    return (x - m) / jnp.sqrt(v + eps)

def _scatter_add(tgt, idx, src, axis=0):
    return tgt.at[idx].add(src)

def _segment_sum(src, seg, n):
    return jax.ops.segment_sum(src, seg, n)
kernel_name = 'mk_xattn_ffn_d1_seqx_r4_bc3799'

def setup_inputs(seed: int=0):
    np.random.seed(seed)
    _w = jnp.asarray

    def _rec_inputs():
        import jax
        import jax.numpy as jnp
        _rk = jax.random.key(seed)
        x = 2.818e-05 + 1 * jax.random.normal(jax.random.fold_in(_rk, 1), (4, 512, 512), jnp.float32)
        _lenS = 512 - jax.random.randint(jax.random.fold_in(_rk, 7), (4,), 0, max(1, 512 // 4) + 1, jnp.int32)
        _lenS2 = 512 - jax.random.randint(jax.random.fold_in(_rk, 8), (4,), 0, max(1, 512 // 4) + 1, jnp.int32)
        _ctx_1024P = jax.random.normal(jax.random.fold_in(_rk, 11), (4, 16, 256), jnp.float32)
        _ctx_1024c = jax.random.dirichlet(jax.random.fold_in(_rk, 511), 0.3 * jnp.ones((16,), jnp.float32), (4, 512))
        _ctx_1024t = jnp.einsum('bsk,bkd->bsd', _ctx_1024c, _ctx_1024P)
        _ctx_1024t = _ctx_1024t * jax.lax.rsqrt(jnp.mean(jnp.square(_ctx_1024t)) + 1e-12) * 0.953939
        ctx_1024 = 7.22013e-05 + 1.00017 * (_ctx_1024t + 0.3 * jax.random.normal(jax.random.fold_in(_rk, 611), (4, 512, 256), jnp.float32))
        return (x, ctx_1024)
    x, ctx_1024 = _rec_inputs()

    def _L0_xattn_setup():
        import jax, jax.numpy as jnp
        import numpy as np
        B_, L_, D_MODEL = (4, 512, 256)
        D_STATE, D_CONV, EXPAND = (16, 4, 2)
        D_INNER = EXPAND * D_MODEL
        DT_RANK = (D_MODEL + 15) // 16

        def silu(x):
            return x * jax.nn.sigmoid(x)
        key = jax.random.key(seed)
        ks = jax.random.split(key, 10)
        f32 = jnp.float32
        hidden_states = jax.random.normal(ks[0], (B_, L_, D_MODEL), dtype=f32)
        z = jax.random.normal(ks[1], (B_, D_INNER, L_), dtype=f32)
        in_proj_w = jax.random.normal(ks[2], (D_INNER, D_MODEL), dtype=f32) * 0.02
        conv_w = jax.random.normal(ks[3], (D_INNER, 1, D_CONV), dtype=f32) * 0.1
        conv_b = jax.random.normal(ks[4], (D_INNER,), dtype=f32) * 0.02
        x_proj_w = jax.random.normal(ks[5], (DT_RANK + 2 * D_STATE, D_INNER), dtype=f32) * 0.02
        dt_proj_w = jax.random.uniform(ks[6], (D_INNER, DT_RANK), dtype=f32, minval=-DT_RANK ** (-0.5), maxval=DT_RANK ** (-0.5))
        dt = jnp.exp(jax.random.uniform(ks[7], (D_INNER,), dtype=f32, minval=np.log(0.001), maxval=np.log(0.1)))
        dt_proj_b = jnp.log(jnp.expm1(dt))
        A_log = jnp.log(jnp.broadcast_to(jnp.arange(1, D_STATE + 1, dtype=f32), (D_INNER, D_STATE)))
        D = jnp.ones((D_INNER,), f32)
        return {'hidden_states': hidden_states, 'z': z, 'in_proj_w': in_proj_w, 'conv_w': conv_w, 'conv_b': conv_b, 'x_proj_w': x_proj_w, 'dt_proj_w': dt_proj_w, 'dt_proj_b': dt_proj_b, 'A_log': A_log, 'D': D}
    _L0_xattn_all = _L0_xattn_setup()
    _L0_xattn_in = {k: v for k, v in _L0_xattn_all.items() if k in ('in_proj_w', 'conv_w', 'conv_b', 'x_proj_w', 'dt_proj_w', 'dt_proj_b', 'A_log', 'D')}
    del _L0_xattn_all

    def _L0_ffn_setup():
        import jax, jax.numpy as jnp
        import numpy as np
        E, K, H, I = (64, 6, 512, 352)
        NS = 2
        IS = NS * I
        CAP = 64
        T_TOKENS = (1, 256)
        SCALE = 0.02

        def _moe_infer(x, gate_w, w_gate, w_up, w_down):
            T = x.shape[0]
            TK = T * K
            logits = x @ gate_w.T
            scores = jax.nn.softmax(logits, axis=-1)
            topk_w, topk_i = jax.lax.top_k(scores, K)
            flat_i = topk_i.reshape(-1)
            flat_w = topk_w.reshape(-1)
            token_ids = jnp.arange(TK, dtype=jnp.int32) // K
            order = jnp.argsort(flat_i)
            sorted_e = flat_i[order]
            counts = jnp.bincount(flat_i, length=E)
            starts = jnp.concatenate([jnp.zeros((1,), counts.dtype), jnp.cumsum(counts)[:-1]])
            pos_sorted = jnp.arange(TK) - starts[sorted_e]
            pos = jnp.zeros((TK,), jnp.int32).at[order].set(pos_sorted.astype(jnp.int32))
            valid = pos < CAP
            slot = jnp.where(valid, pos, CAP)
            buf = jnp.zeros((E, CAP + 1, H), x.dtype).at[flat_i, slot].set(x[token_ids])
            g = jnp.einsum('ech,ehi->eci', buf, w_gate)
            u = jnp.einsum('ech,ehi->eci', buf, w_up)
            y = jnp.einsum('eci,eih->ech', jax.nn.silu(g) * u, w_down)
            out_slots = y[flat_i, slot] * (flat_w * valid)[:, None]
            return out_slots.reshape(T, K, H).sum(axis=1)
        key = jax.random.key(seed)
        ks = jax.random.split(key, 8)
        f32 = jnp.float32
        return {'hidden_states': jax.random.normal(ks[0], (*T_TOKENS, H), f32), 'gate_w': jax.random.normal(ks[1], (E, H), f32) * SCALE, 'w_gate': jax.random.normal(ks[2], (E, H, I), f32) * SCALE, 'w_up': jax.random.normal(ks[3], (E, H, I), f32) * SCALE, 'w_down': jax.random.normal(ks[4], (E, I, H), f32) * SCALE, 'sw_gate': jax.random.normal(ks[5], (H, IS), f32) * SCALE, 'sw_up': jax.random.normal(ks[6], (H, IS), f32) * SCALE, 'sw_down': jax.random.normal(ks[7], (IS, H), f32) * SCALE}
    _L0_ffn_all = _L0_ffn_setup()
    _L0_ffn_in = {k: v for k, v in _L0_ffn_all.items() if k in ('gate_w', 'w_gate', 'w_up', 'w_down', 'sw_gate', 'sw_up', 'sw_down')}
    del _L0_ffn_all
    return {'x': x, 'ctx_1024': ctx_1024, 'L0_xattn_in_proj_w': _L0_xattn_in['in_proj_w'], 'L0_xattn_conv_w': _L0_xattn_in['conv_w'], 'L0_xattn_conv_b': _L0_xattn_in['conv_b'], 'L0_xattn_x_proj_w': _L0_xattn_in['x_proj_w'], 'L0_xattn_dt_proj_w': _L0_xattn_in['dt_proj_w'], 'L0_xattn_dt_proj_b': _L0_xattn_in['dt_proj_b'], 'L0_xattn_A_log': _L0_xattn_in['A_log'], 'L0_xattn_D': _L0_xattn_in['D'], 'L0_ffn_gate_w': _L0_ffn_in['gate_w'], 'L0_ffn_w_gate': _L0_ffn_in['w_gate'], 'L0_ffn_w_up': _L0_ffn_in['w_up'], 'L0_ffn_w_down': _L0_ffn_in['w_down'], 'L0_ffn_sw_gate': _L0_ffn_in['sw_gate'], 'L0_ffn_sw_up': _L0_ffn_in['sw_up'], 'L0_ffn_sw_down': _L0_ffn_in['sw_down']}

def reference(x, ctx_1024, L0_xattn_in_proj_w, L0_xattn_conv_w, L0_xattn_conv_b, L0_xattn_x_proj_w, L0_xattn_dt_proj_w, L0_xattn_dt_proj_b, L0_xattn_A_log, L0_xattn_D, L0_ffn_gate_w, L0_ffn_w_gate, L0_ffn_w_up, L0_ffn_w_down, L0_ffn_sw_gate, L0_ffn_sw_up, L0_ffn_sw_down):
    import jax
    import jax.numpy as jnp

    def _L0_xattn_ref(hidden_states, z, in_proj_w, conv_w, conv_b, x_proj_w, dt_proj_w, dt_proj_b, A_log, D):
        import jax, jax.numpy as jnp
        import numpy as np
        B_, L_, D_MODEL = (4, 512, 256)
        D_STATE, D_CONV, EXPAND = (16, 4, 2)
        D_INNER = EXPAND * D_MODEL
        DT_RANK = (D_MODEL + 15) // 16

        def silu(x):
            return x * jax.nn.sigmoid(x)
        Bsz, L, _ = hidden_states.shape
        d_inner, _, d_conv = conv_w.shape
        dt_rank = dt_proj_w.shape[1]
        d_state = A_log.shape[1]
        x = jnp.einsum('bld,ed->bel', hidden_states, in_proj_w)
        xc = jax.lax.conv_general_dilated(x, conv_w, window_strides=(1,), padding=[(d_conv - 1, 0)], feature_group_count=d_inner, dimension_numbers=('NCH', 'OIH', 'NCH'))
        x = silu(xc + conv_b[None, :, None])
        x_dbl = jnp.einsum('bdl,ed->bel', x, x_proj_w)
        dt_low, Bm, Cm = jnp.split(x_dbl, [dt_rank, dt_rank + d_state], axis=1)
        dt = jnp.einsum('brl,dr->bdl', dt_low, dt_proj_w)
        dt = jax.nn.softplus(dt + dt_proj_b[None, :, None])
        A = -jnp.exp(A_log)
        dt_t = jnp.moveaxis(dt, -1, 0)
        B_t = jnp.moveaxis(Bm, -1, 0)
        C_t = jnp.moveaxis(Cm, -1, 0)
        u_t = jnp.moveaxis(x, -1, 0)

        def step(state, inp):
            d, b, c, u = inp
            dA = jnp.exp(d[..., None] * A)
            state = state * dA + (d * u)[..., None] * b[:, None, :]
            y = jnp.einsum('bdn,bn->bd', state, c)
            return (state, y)
        state0 = jnp.zeros((Bsz, d_inner, d_state), x.dtype)
        _, ys = jax.lax.scan(step, state0, (dt_t, B_t, C_t, u_t))
        y = jnp.moveaxis(ys, 0, 2)
        y = y + D[None, :, None] * x
        y = y * silu(z)
        return jnp.swapaxes(y, 1, 2)

    def _L0_ffn_ref(hidden_states, gate_w, w_gate, w_up, w_down, sw_gate, sw_up, sw_down):
        import jax, jax.numpy as jnp
        import numpy as np
        E, K, H, I = (64, 6, 512, 352)
        NS = 2
        IS = NS * I
        CAP = 64
        T_TOKENS = (1, 256)
        SCALE = 0.02

        def _moe_infer(x, gate_w, w_gate, w_up, w_down):
            T = x.shape[0]
            TK = T * K
            logits = x @ gate_w.T
            scores = jax.nn.softmax(logits, axis=-1)
            topk_w, topk_i = jax.lax.top_k(scores, K)
            flat_i = topk_i.reshape(-1)
            flat_w = topk_w.reshape(-1)
            token_ids = jnp.arange(TK, dtype=jnp.int32) // K
            order = jnp.argsort(flat_i)
            sorted_e = flat_i[order]
            counts = jnp.bincount(flat_i, length=E)
            starts = jnp.concatenate([jnp.zeros((1,), counts.dtype), jnp.cumsum(counts)[:-1]])
            pos_sorted = jnp.arange(TK) - starts[sorted_e]
            pos = jnp.zeros((TK,), jnp.int32).at[order].set(pos_sorted.astype(jnp.int32))
            valid = pos < CAP
            slot = jnp.where(valid, pos, CAP)
            buf = jnp.zeros((E, CAP + 1, H), x.dtype).at[flat_i, slot].set(x[token_ids])
            g = jnp.einsum('ech,ehi->eci', buf, w_gate)
            u = jnp.einsum('ech,ehi->eci', buf, w_up)
            y = jnp.einsum('eci,eih->ech', jax.nn.silu(g) * u, w_down)
            out_slots = y[flat_i, slot] * (flat_w * valid)[:, None]
            return out_slots.reshape(T, K, H).sum(axis=1)
        orig_shape = hidden_states.shape
        x = hidden_states.reshape(-1, orig_shape[-1])
        y = _moe_infer(x, gate_w, w_gate, w_up, w_down).reshape(orig_shape)
        shared = jax.nn.silu(hidden_states @ sw_gate) * (hidden_states @ sw_up) @ sw_down
        return y + shared
    x = x + _L0_xattn_ref(ctx_1024, _layernorm(x, axis=-1), L0_xattn_in_proj_w, L0_xattn_conv_w, L0_xattn_conv_b, L0_xattn_x_proj_w, L0_xattn_dt_proj_w, L0_xattn_dt_proj_b, L0_xattn_A_log, L0_xattn_D)
    x = x + _L0_ffn_ref(_layernorm(x, axis=-1), L0_ffn_gate_w, L0_ffn_w_gate, L0_ffn_w_up, L0_ffn_w_down, L0_ffn_sw_gate, L0_ffn_sw_up, L0_ffn_sw_down)
    return x

_drawn_inputs = setup_inputs


def setup_inputs(seed=0):
    import zlib

    import numpy as np

    out = dict(_drawn_inputs(seed))
    spreads = {'L0_xattn_D': (1.0, 0.6)}
    factors = {'ctx_1024': 2.894,
     'L0_xattn_in_proj_w': 2.899,
     'L0_xattn_conv_w': 2.957,
     'L0_xattn_conv_b': 8.0,
     'L0_xattn_x_proj_w': 8.0,
     'L0_xattn_dt_proj_w': 8.0,
     'L0_xattn_dt_proj_b': 8.0,
     'L0_xattn_A_log': 8.0,
     'L0_ffn_gate_w': 8.0,
     'L0_ffn_w_gate': 7.876,
     'L0_ffn_w_up': 7.596,
     'L0_ffn_w_down': 7.612,
     'L0_ffn_sw_gate': 8.0,
     'L0_ffn_sw_up': 8.0,
     'L0_ffn_sw_down': 8.0}
    for name, (base, spread) in spreads.items():
        noise = np.random.default_rng([zlib.crc32(name.encode()), seed]).standard_normal(out[name].shape)
        drawn = base * np.exp(spread * noise) if base else spread * noise
        out[name] = jnp.asarray(drawn.astype(out[name].dtype))
    for name, factor in factors.items():
        out[name] = (out[name] * factor).astype(out[name].dtype)
    return out
```

```python
from contextlib import ExitStack

import concourse.bass as bass
from concourse import mybir

F32 = mybir.dt.float32
BF16 = mybir.dt.bfloat16
U32 = mybir.dt.uint32
ALU = mybir.AluOpType
ACT = mybir.ActivationFunctionType
AX_X = mybir.AxisListType.X

P = 128
B, L, H = 4, 512, 512
DM, DI, NS, DR = 256, 512, 16, 16
TAPS = 4
E, K, I, CAP = 64, 6, 352, 64
IS = 704
T = B * L
EPS = 1e-5
DC = DI // P
LT = L // P
HC = H // P
NB = 2
NG = NS // NB
STEPS = NG * DC
ISC = [P] * (IS // P) + [IS % P]
NI = len(ISC)
NPAIR = E // 2
IC = 3
IREST = I - 2 * P
TRASH = T
SERIES_BELOW = 0.03


def build(nc, x, ctx_1024, in_proj_w, conv_w, conv_b, x_proj_w, dt_proj_w, dt_proj_b, A_log, D,
          gate_w, w_gate, w_up, w_down, sw_gate, sw_up, sw_down, out):
    bc_dram = nc.dram_tensor("bc_rows", [B, 2 * NS, L], F32, kind="Internal").ap()
    xn_dram = nc.dram_tensor("xn_rows", [T + CAP, H], F32, kind="Internal").ap()
    slot_dram = nc.dram_tensor("slot_table", [E * CAP, 2], F32, kind="Internal").ap()

    with ExitStack() as ctx:
        ctx.enter_context(nc.allow_non_contiguous_dma(reason="small parameter loads"))

        def sb(name, shape, dt=F32):
            return ctx.enter_context(nc.sbuf_tensor(name, shape, dt))

        def sem(name):
            return ctx.enter_context(nc.semaphore(name))

        GW = 2 * HC * I
        DWN = 2 * IC * H
        PAIRW = 2 * GW + DWN
        arena = sb("arena", [P, 2 * PAIRW])
        at = [0]

        def carve(t, words):
            a = t[:, at[0]:at[0] + words]
            at[0] += words
            return a

        dA = [carve(arena, NB * L).rearrange("p (n l) -> p n l", n=NB) for _ in range(2)]
        S = [carve(arena, NB * L).rearrange("p (n l) -> p n l", n=NB) for _ in range(3)]
        Brep = [carve(arena, NB * L).rearrange("p (n l) -> p n l", n=NB) for _ in range(2)]
        Crep = [carve(arena, NB * L).rearrange("p (n l) -> p n l", n=NB) for _ in range(2)]
        dt = [carve(arena, DC * L).rearrange("p (c l) -> p c l", c=DC) for _ in range(2)]
        dtu = [carve(arena, DC * L).rearrange("p (c l) -> p c l", c=DC) for _ in range(2)]
        assert at[0] <= 2 * PAIRW
        at[0] = 0
        wg, wu, wd = [], [], []
        for j in range(2):
            wg.append(carve(arena, GW).rearrange("p (e c i) -> p e c i", e=2, c=HC))
            wu.append(carve(arena, GW).rearrange("p (e c i) -> p e c i", e=2, c=HC))
            wd.append(carve(arena, DWN).rearrange("p (e c h) -> p e c h", e=2, c=IC))

        XP = L + TAPS - 1
        prep = sb("prep", [P, DC * L + DC * XP + LT * DM + 2 * L])
        at[0] = 0
        u = carve(prep, DC * L).rearrange("p (c l) -> p c l", c=DC)
        xpad = carve(prep, DC * XP).rearrange("p (c l) -> p c l", c=DC)
        cin = carve(prep, LT * DM).rearrange("p (t d) -> p t d", t=LT)
        ctxT = carve(prep, 2 * L).rearrange("p (m l) -> p m l", m=2)
        at[0] = 0
        xg, xgT, hh, hT, ys = [], [], [], [], []
        for j in range(2):
            xg.append(carve(prep, H))
            xgT.append(carve(prep, H).rearrange("p (c t) -> p c t", c=HC))
            hh.append(carve(prep, IC * P))
            hT.append(carve(prep, IC * P).rearrange("p (c t) -> p c t", c=IC))
            ys.append(carve(prep, H))
        tab = carve(prep, 2 * P)[0:NPAIR]
        ids = carve(prep, 3 * NPAIR).bitcast(U32).rearrange("p (q k) -> p q k", k=3)
        wts = carve(prep, NPAIR)

        xb = [sb(f"xb{j}", [P, LT, H]) for j in range(2)]
        zx = sb("zx", [P, LT, H])
        zT = sb("zT", [P, LT, DI])
        xnT = sb("xnT", [P, HC, L])
        hs = sb("hs", [P, NI, L])
        swg = sb("swg", [P, HC, IS])
        swu = sb("swu", [P, HC, IS])
        swd = sb("swd", [P, NI, H])
        bt1 = sb("bt1", [P, DC, L])
        bt2 = sb("bt2", [P, DC, L])
        tg = [sb(f"tg{j}", [P, L]) for j in range(2)]
        winT = sb("winT", [P, 2, DI])
        xpT = sb("xpT", [P, DC, DR + 2 * NS])
        dtwT = sb("dtwT", [DR, DI])
        xdbl = sb("xdbl", [DR + 2 * NS, L])
        gwT = sb("gwT", [P, HC, E])
        ident = sb("ident", [P, P])
        ltri = sb("ltri", [P, P], BF16)
        ones = sb("ones", [P, P], BF16)
        vec = sb("vec", [P, 3 * DC])
        cw = sb("cw", [P, DC, TAPS])
        An = sb("An", [P, DC, NS])
        stats = sb("stats", [P, LT, 6])
        mv = sb("mv", [P, LT, 2])
        gsc = sb("gsc", [P, LT, 2])
        mhalf = sb("mhalf", [P, LT])
        iota_e = sb("iota_e", [P, E])
        tokid = sb("tokid", [P, B * LT])
        csum = sb("csum", [P, E], BF16)
        mask = sb("mask", [P, E], BF16)
        lg = sb("lg", [P, E])
        m8 = sb("m8", [P, 8])
        i8 = sb("i8", [P, 8], U32)
        i8f = sb("i8f", [P, K])
        negm = sb("negm", [P, 1])
        ssum = sb("ssum", [P, 1])
        e6 = sb("e6", [P, K])
        oh = sb("oh", [P, K, E])
        ohp = sb("ohp", [P, K, E])
        posk = sb("posk", [P, K])
        slotf = sb("slotf", [P, K])
        over = sb("over", [P, K])
        slotu = sb("slotu", [P, B * LT, K], U32)
        rec = sb("rec", [P, B * LT, K, 2])
        idxg = [sb(f"idxg{j}", [P, 1], U32) for j in range(2)]
        idxs = [sb(f"idxs{j}", [CAP, 2], U32) for j in range(2)]
        wcol = [sb(f"wcol{j}", [P, 1]) for j in range(2)]
        ps = ctx.enter_context(nc.psum_tensor("ps", [P, 8, 512], F32))
        ps_y = ps[:, 0:4, :]

        raw_win = zx[:, 0:2, :].rearrange("p t (c d) -> p (t c) d", d=DM)
        raw_gw = zT[0:E, 0, :]
        raw_xp = zT[0:DR + 2 * NS, 1, :]
        raw_dtw = zT[:, 2, 0:DC * DR].rearrange("p (c r) -> p c r", c=DC)
        raw_vec = zT[0:3 * DC, 3, 0:P]
        zeros = bt2[0:CAP, 0, :]
        initrow = bt2[0:E, 1, 0:2 * CAP].rearrange("e (c t) -> e c t", t=2)

        names = """par_in sw_in const_set a_exp iota_set init_in pre_t pre_ev
            ctx_in0 ctx_in1 x_in0 x_in1 bc_st rep_in0 rep_in1 xn_st out_st scattered
            ctxT_mm ctxT_ready inproj_mm xpad_ready conv_done tanh_ready u_ready xdbl_mm xdbl_ready
            dt_mm xs_done xm_ready e_ready ser_chain ser_ready l_ready dt_ready du_ready duT_done
            dA_done dbu_done scan_done cs_done yT_done
            var_ready rstd_ready zin_ready gth_ready zg_ready zT_mm zT_ready yz_done xn_ready xnT_mm xnT_ready
            lg_mm lg_ready m_ready ex_ready mask_ready pos_mm slot_ready
            gu_mm sth_ready sa_ready hs_ready dn_mm ob_ready dve
            held tab_in tab_mm ids_ready idx_ready w_ready xg_in0 xg_in1 xgT_mm xgT_ready
            gu_in0 gu_in1 wd_in0 wd_in1 egu_mm silu_ready h_ready hT_mm hT_ready y_mm y_ready
            sc_even sc_odd pad_set""".split()
        s = {n: sem(n) for n in names}
        rep_in = [s["rep_in0"], s["rep_in1"]]
        x_in = [s["x_in0"], s["x_in1"]]
        xg_in = [s["xg_in0"], s["xg_in1"]]
        gu_in = [s["gu_in0"], s["gu_in1"]]
        wd_in = [s["wd_in0"], s["wd_in1"]]

        def side(b):
            work = [("xnT", b - 1, None)] if b >= 1 else []
            work += [("gate", b, None)]
            if b >= 1:
                work += [("router", b - 1, t) for t in range(LT)]
                work += [("shared", b - 1, c) for c in range(NI)]
                work += [("down", b - 1, t) for t in range(LT)]
            if b + 1 < B:
                work += [(k, b + 1, c) for k, c in PREP]
            return work

        PREP = ([("ctx", None)] + [("inproj", c) for c in range(DC)] + [("silu", None), ("xdbl", None)]
                + [("dt", c) for c in range(DC)] + [("softplus", None)])
        SCHEDULE = [(k, 0, c) for k, c in PREP]
        for b in range(B):
            SCHEDULE.append(("head", b, None))
            work = side(b)
            for step in range(STEPS):
                SCHEDULE.append(("step", b, step))
                done = len(work) * step // STEPS
                SCHEDULE += work[done:len(work) * (step + 1) // STEPS]
            SCHEDULE.append(("tail", b, None))
        SCHEDULE.append(("xnT", B - 1, None))
        SCHEDULE += [("router", B - 1, t) for t in range(LT)]
        SCHEDULE += [("shared", B - 1, c) for c in range(NI)]
        SCHEDULE += [("down", B - 1, t) for t in range(LT)]

        def gi(b, g):
            return b * NG + g

        block = ctx.enter_context(nc.Block())

        def gate_up(sp, q, j):
            for w, dst in ((w_gate, wg), (w_up, wu)):
                src = w.rearrange("(q e) (p c) i -> q p e (c i)", e=2, c=HC)
                sp.dma_start(dst[j].rearrange("p e c i -> p e (c i)"), pick(src, q)).then_inc(gu_in[j], 16)

        def pick(a, q):
            return a[bass.ds(q, 1)].rearrange("o p e f -> (o p) e f") if not isinstance(q, int) else a[q]

        def down(sp, q, j):
            head = w_down[:, 0:2 * P, :].rearrange("(q e) (p c) h -> q p e (c h)", e=2, c=2)
            rest = w_down[:, 2 * P:I, :].rearrange("(q e) p h -> q p e h", e=2)
            sp.dma_start(wd[j][:, :, 0:2, :].rearrange("p e c h -> p e (c h)"), pick(head, q)).then_inc(wd_in[j], 16)
            sp.dma_start(wd[j][0:IREST, :, 2, :], pick(rest, q)).then_inc(wd_in[j], 16)

        def weights(sp, q, j):
            gate_up(sp, q, j)
            sp.wait_ge(s["pad_set"], 2)
            down(sp, q, j)

        @block.sync
        def _(sp):
            def load(dst, src, sm):
                return sp.dma_start(dst, src).then_inc(sm, 16)

            load(cin, ctx_1024[0].rearrange("(t p) d -> p t d", p=P), s["ctx_in0"])
            load(raw_win, in_proj_w.rearrange("(c p) d -> p c d", p=P), s["par_in"])
            load(raw_xp, x_proj_w, s["par_in"])
            load(raw_dtw, dt_proj_w.rearrange("(c p) r -> p c r", p=P), s["par_in"])
            load(raw_vec[0:DC], conv_b.rearrange("(c p) -> c p", p=P), s["par_in"])
            load(raw_vec[DC:2 * DC], dt_proj_b.rearrange("(c p) -> c p", p=P), s["par_in"])
            load(raw_vec[2 * DC:3 * DC], D.rearrange("(c p) -> c p", p=P), s["par_in"])
            load(cw[:], conv_w.rearrange("(c p) o k -> p c (o k)", p=P), s["par_in"])
            load(An[:], A_log.rearrange("(c p) n -> p c n", p=P), s["par_in"])
            load(raw_gw, gate_w, s["par_in"])
            load(xb[0][:], x[0].rearrange("(t p) c -> p t c", p=P), x_in[0])
            sp.wait_ge(s["const_set"], 1)
            load(xn_dram[T:T + CAP, :], zeros, s["init_in"])
            load(out[T:T + CAP, :], zeros, s["init_in"])
            load(slot_dram.rearrange("(e c) t -> e (c t)", e=E),
                 initrow.rearrange("e c t -> e (c t)"), s["init_in"])
            load(swg[:], sw_gate.rearrange("(p c) i -> p c i", c=HC), s["sw_in"])
            load(swu[:], sw_up.rearrange("(p c) i -> p c i", c=HC), s["sw_in"])
            load(swd[:, 0:NI - 1, :], sw_down[0:(NI - 1) * P].rearrange("(c p) h -> p c h", p=P), s["sw_in"])
            load(swd[0:IS % P, NI - 1, :], sw_down[(NI - 1) * P:IS], s["sw_in"])

            def rep(b, g):
                n = gi(b, g)
                if g == 0:
                    sp.wait_ge(s["bc_st"], 16 * (b + 1))
                if n >= 2:
                    sp.wait_ge(s["dbu_done"], DC * (n - 1))
                    sp.wait_ge(s["cs_done"], DC * (n - 1))
                for dst, row in ((Brep, 0), (Crep, NS)):
                    src = bc_dram[b:b + 1, row + NB * g:row + NB * (g + 1), :].to_broadcast([P, NB, L])
                    load(dst[n % 2], src, rep_in[n % 2])

            for kind, b, c in SCHEDULE:
                if kind == "ctx" and b >= 1:
                    sp.wait_ge(s["ctxT_mm"], 2 * b)
                    load(cin, ctx_1024[b].rearrange("(t p) d -> p t d", p=P), s["ctx_in0"])
                elif kind == "xdbl":
                    sp.wait_ge(s["xdbl_ready"], b + 1)
                    load(bc_dram[b], xdbl[DR:DR + 2 * NS, :], s["bc_st"])
                    if b == 0:
                        rep(0, 0)
                        rep(0, 1)
                elif kind == "step" and c % DC == DC - 1:
                    n = gi(b, c // DC) + 2
                    if n < B * NG:
                        rep(n // NG, n % NG)
                elif kind == "head" and b + 1 < B:
                    if b == 0:
                        load(xb[1][:], x[1].rearrange("(t p) c -> p t c", p=P), x_in[1])
                elif kind == "down" and c == LT - 1:
                    sp.wait_ge(s["ob_ready"], LT * (b + 1))
                    load(out[b * L:(b + 1) * L].rearrange("(t p) c -> p t c", p=P), xb[b % 2][:], s["out_st"])
                    if b + 2 < B:
                        sp.wait_ge(s["out_st"], 16 * (b + 1))
                        load(xb[b % 2][:], x[b + 2].rearrange("(t p) c -> p t c", p=P), x_in[b % 2])
                elif kind == "tail":
                    sp.wait_ge(s["xn_ready"], LT * (b + 1))
                    load(xn_dram[b * L:(b + 1) * L].rearrange("(t p) c -> p t c", p=P), zx[:], s["xn_st"])
                    if b == B - 1:
                        sp.wait_ge(s["yT_done"], B * STEPS)
                        sp.wait_ge(s["dA_done"], B * STEPS)
                        for j in range(2):
                            weights(sp, j, j)
            sp.wait_ge(s["scattered"], 16 * B * LT * K)
            load(tab[:], slot_dram.rearrange("(q c) t -> q (c t)", q=NPAIR), s["tab_in"])

            def free_then_load(i, j):
                sp.wait_ge(s["egu_mm"], 2 * i + j - 1)
                gate_up(sp, 2 * i + j, j)
                sp.wait_ge(s["y_mm"], 2 * i + j - 1)
                down(sp, 2 * i + j, j)

            with sp.Fori(1, NPAIR // 2) as i:
                for j in range(2):
                    free_then_load(i, j)
            sp.wait_ge(s["sc_odd"], 16 * NPAIR)
            sp.wait_ge(s["sc_even"], 16 * NPAIR)
            sp.wait_ge(s["out_st"], 16 * B)
            sp.wait_ge(s["xn_st"], 16 * B)
            sp.wait_ge(s["init_in"], 16 * 3)

        @block.tensor
        def _(pe):
            freed = {}

            def claim(bank):
                if bank in freed:
                    pe.wait_ge(*freed[bank])

            def transpose(dst, src, **kw):
                k = src.shape[0]
                return nc.tensor.matmul(dst, src, ident[0:k, 0:k], is_transpose=True, **kw)

            def flip(bank, cols, srcs, **kw):
                for n, a in enumerate(srcs):
                    m, k = a.shape[1], a.shape[0]
                    last = transpose(ps[0:m, bank, cols + n * k:cols + (n + 1) * k], a, start=True, stop=True)
                return last

            pe.wait_ge(s["const_set"], 3)
            pe.wait_ge(s["par_in"], 16 * 9)
            for m in range(2):
                flip(4 + m, 0, [raw_win[:, c, m * P:(m + 1) * P] for c in range(DC)]).then_inc(s["pre_t"], 1)
            flip(6, 0, [raw_gw[:, c::HC] for c in range(HC)]).then_inc(s["pre_t"], 1)
            flip(7, 0, [raw_xp[:, c * P:(c + 1) * P] for c in range(DC)])
            flip(7, 256, [raw_vec]).then_inc(s["pre_t"], 1)
            pe.wait_ge(s["pre_ev"], 2)
            flip(4, 0, [raw_dtw[:, c, :] for c in range(DC)]).then_inc(s["pre_t"], 1)
            freed.update({4: (s["pre_ev"], 6), 5: (s["pre_ev"], 6), 6: (s["pre_ev"], 6), 7: (s["pre_ev"], 6)})
            pe.wait_ge(s["pre_ev"], 6)

            for kind, b, c in SCHEDULE:
                if kind == "ctx":
                    pe.wait_ge(s["ctx_in0"], 16 * (b + 1))
                    for m in range(2):
                        claim(4 + m)
                        flip(4 + m, 0, [cin[:, t, m * P:(m + 1) * P] for t in range(LT)]).then_inc(s["ctxT_mm"], 1)
                        freed[4 + m] = (s["ctxT_ready"], 2 * b + m + 1)
                elif kind == "inproj":
                    bank = 4 + c % 2
                    claim(bank)
                    pe.wait_ge(s["ctxT_ready"], 2 * b + 2)
                    for m in range(2):
                        mm = nc.tensor.matmul(ps[:, bank, :], winT[:, m, c * P:(c + 1) * P], ctxT[:, m, :],
                                              start=(m == 0), stop=(m == 1))
                    mm.then_inc(s["inproj_mm"], 1)
                    freed[bank] = (s["xpad_ready"], DC * b + c + 1)
                elif kind == "xdbl":
                    claim(4)
                    pe.wait_ge(s["u_ready"], DC * (b + 1))
                    for k in range(DC):
                        mm = nc.tensor.matmul(ps[0:DR + 2 * NS, 4, :], xpT[:, k, :], u[:, k, :],
                                              start=(k == 0), stop=(k == DC - 1))
                    mm.then_inc(s["xdbl_mm"], 1)
                    freed[4] = (s["xdbl_ready"], b + 1)
                elif kind == "dt":
                    bank = 5 - c % 2
                    claim(bank)
                    pe.wait_ge(s["xdbl_ready"], b + 1)
                    nc.tensor.matmul(ps[:, bank, :], dtwT[:, c * P:(c + 1) * P], xdbl[0:DR, :],
                                     start=True, stop=True).then_inc(s["dt_mm"], 1)
                    freed[bank] = (s["xs_done"], DC * b + c + 1)
                elif kind == "head":
                    pe.wait_ge(s["du_ready"], DC * (b + 1))
                    for t in range(LT):
                        if b >= 1:
                            pe.wait_ge(s["yz_done"], LT * (b - 1) + t + 1)
                        for k in range(DC):
                            mm = transpose(ps_y[:, t, k * P:(k + 1) * P], bt2[:, k, t * P:(t + 1) * P],
                                           start=(k == 0), stop=False, skip_group_check=True)
                    mm.then_inc(s["duT_done"], 1)
                elif kind == "step":
                    q = b * STEPS + c
                    k = c % DC
                    pe.wait_ge(s["cs_done"], q + 1)
                    for n in range(NB):
                        for t in range(LT):
                            mm = transpose(ps_y[:, t, k * P:(k + 1) * P], S[q % 3][:, n, t * P:(t + 1) * P],
                                           start=False, stop=(c >= STEPS - DC and n == NB - 1),
                                           skip_group_check=True)
                    mm.then_inc(s["yT_done"], 1)
                elif kind == "gate":
                    for t in range(LT):
                        bank = 4 + t % 2
                        claim(bank)
                        pe.wait_ge(s["zg_ready"], LT * (b + 1))
                        flip(bank, 0, [zx[:, k, t * P:(t + 1) * P] for k in range(DC)]).then_inc(s["zT_mm"], 1)
                        freed[bank] = (s["zT_ready"], LT * b + t + 1)
                elif kind == "xnT":
                    pe.wait_ge(s["xn_ready"], LT * (b + 1))
                    for k in range(HC):
                        bank = 4 + k % 2
                        claim(bank)
                        flip(bank, 0, [zx[:, t, k::HC] for t in range(LT)]).then_inc(s["xnT_mm"], 1)
                        freed[bank] = (s["xnT_ready"], HC * b + k + 1)
                elif kind == "router":
                    n = LT * b + c
                    pe.wait_ge(s["xnT_ready"], HC * (b + 1))
                    claim(4)
                    for k in range(HC):
                        mm = nc.tensor.matmul(ps[:, 4, 0:E], xnT[:, k, c * P:(c + 1) * P], gwT[:, k, :],
                                              start=(k == 0), stop=(k == HC - 1))
                    mm.then_inc(s["lg_mm"], 1)
                    freed[4] = (s["lg_ready"], n + 1)
                    claim(5)
                    pe.wait_ge(s["mask_ready"], n + 1)
                    nc.tensor.matmul(ps[:, 5, 0:E], ltri[:], mask[:], start=True, stop=False)
                    nc.tensor.matmul(ps[:, 5, 0:E], ones[:], csum[:], start=False, stop=True).then_inc(s["pos_mm"], 1)
                    freed[5] = (s["slot_ready"], n + 1)
                elif kind == "shared":
                    m = ISC[c]
                    if b == 0 and c == 0:
                        pe.wait_ge(s["sw_in"], 16 * 4)
                    pe.wait_ge(s["xnT_ready"], HC * (b + 1))
                    for bank, w in ((6, swg), (7, swu)):
                        claim(bank)
                        for k in range(HC):
                            mm = nc.tensor.matmul(ps[0:m, bank, :], w[:, k, c * P:c * P + m], xnT[:, k, :],
                                                  start=(k == 0), stop=(k == HC - 1))
                        freed[bank] = (s["hs_ready"], NI * b + c + 1)
                    mm.then_inc(s["gu_mm"], 1)
                elif kind == "down":
                    bank = 6 + c % 2
                    claim(bank)
                    pe.wait_ge(s["hs_ready"], NI * (b + 1))
                    for k in range(NI):
                        m = ISC[k]
                        mm = nc.tensor.matmul(ps[:, bank, :], hs[0:m, k, c * P:(c + 1) * P], swd[0:m, k, :],
                                              start=(k == 0), stop=(k == NI - 1))
                    mm.then_inc(s["dn_mm"], 1)
                    freed[bank] = (s["ob_ready"], LT * b + c + 1)

            pe.wait_ge(s["tab_in"], 16)
            claim(4)
            claim(5)
            flip(4, 0, [tab[:, 0::2]])
            flip(4, 64, [tab[:, 1::2]])
            flip(4, 128, [tab[:, 0:2 * CAP:2]])
            flip(4, 192, [tab[:, 2 * CAP:4 * CAP:2]]).then_inc(s["tab_mm"], 1)
            for bank in (6, 7):
                claim(bank)
            pe.wait_ge(s["ids_ready"], 4)
            pe.wait_ge(s["yz_done"], LT * B)

            def tokens(i, j, first=False):
                pe.wait_ge(xg_in[j], 16 * (i + 1))
                if not first:
                    pe.wait_ge(s["xgT_ready"], 2 * i + j)
                flip(0, 0, [xg[j][:, k::HC] for k in range(HC)]).then_inc(s["xgT_mm"], 1)

            def gate_up_mm(i, j, first=False):
                pe.wait_ge(s["xgT_ready"], 2 * i + j + 1)
                pe.wait_ge(gu_in[j], 32 * (i + 1))
                if not first:
                    pe.wait_ge(s["h_ready"], 2 * i + j - 1)
                for bank, w in ((2 + j, wg[j]), (4 + j, wu[j])):
                    for k in range(HC):
                        for e in range(2):
                            mm = nc.tensor.matmul(ps[64 * e:64 * e + 64, bank, 0:I],
                                                  xgT[j][:, k, 64 * e:64 * e + 64], w[:, e, k, :],
                                                  start=(k == 0), stop=(k == HC - 1))
                mm.then_inc(s["egu_mm"], 1)

            def acts(i, j, first=False):
                pe.wait_ge(s["h_ready"], 2 * i + j + 1)
                if not first:
                    pe.wait_ge(s["hT_ready"], 2 * i + j)
                flip(1, 0, [hh[j][:, 0:2 * P:2], hh[j][:, 1:2 * P:2], hh[j][:, 2 * P:3 * P]]).then_inc(s["hT_mm"], 1)

            def down_mm(i, j, first=False):
                pe.wait_ge(s["hT_ready"], 2 * i + j + 1)
                pe.wait_ge(wd_in[j], 32 * (i + 1))
                if not first:
                    pe.wait_ge(s["y_ready"], 2 * i + j - 1)
                for k in range(IC):
                    for e in range(2):
                        mm = nc.tensor.matmul(ps[64 * e:64 * e + 64, 6 + j, :], hT[j][:, k, 64 * e:64 * e + 64],
                                              wd[j][:, e, k, :], start=(k == 0), stop=(k == IC - 1))
                mm.then_inc(s["y_mm"], 1)

            tokens(0, 0, True)
            tokens(0, 1)
            gate_up_mm(0, 0, True)
            acts(0, 0, True)
            tokens(1, 0)
            gate_up_mm(0, 1, True)
            down_mm(0, 0, True)
            acts(0, 1)

            def two_pairs(i, first=False):
                tokens(i, 1)
                gate_up_mm(i, 0)
                down_mm(i - 1, 1, first)
                acts(i, 0)
                tokens(i + 1, 0)
                gate_up_mm(i, 1)
                down_mm(i, 0)
                acts(i, 1)

            two_pairs(1, True)
            with pe.Fori(2, NPAIR // 2 - 1) as i:
                two_pairs(i)
            i = NPAIR // 2 - 1
            tokens(i, 1)
            gate_up_mm(i, 0)
            down_mm(i - 1, 1)
            acts(i, 0)
            gate_up_mm(i, 1)
            down_mm(i, 0)
            acts(i, 1)
            down_mm(i, 1)

        @block.scalar
        def _(act):
            def copy(dst, src, sm):
                nc.scalar.copy(dst, src).then_inc(sm, 1)

            act.wait_ge(s["par_in"], 16 * 9)
            nc.scalar.activation(An[:], An[:], ACT.Exp).then_inc(s["a_exp"], 1)
            act.wait_ge(s["pre_t"], 2)
            for m in range(2):
                copy(winT[:, m, :], ps[:, 4 + m, :], s["pre_ev"])
            act.wait_ge(s["pre_t"], 3)
            copy(gwT[:], ps[:, 6, 0:HC * E].rearrange("p (c e) -> p c e", c=HC), s["pre_ev"])
            act.wait_ge(s["pre_t"], 4)
            w = DR + 2 * NS
            copy(xpT[:], ps[:, 7, 0:DC * w].rearrange("p (c r) -> p c r", c=DC), s["pre_ev"])
            copy(vec[:], ps[:, 7, 256:256 + 3 * DC], s["pre_ev"])
            act.wait_ge(s["pre_t"], 5)
            copy(dtwT[:], ps[0:DR, 4, :], s["pre_ev"])

            used = {}

            for kind, b, c in SCHEDULE:
                if kind == "ctx":
                    for m in range(2):
                        act.wait_ge(s["ctxT_mm"], 2 * b + m + 1)
                        if b >= 1:
                            act.wait_ge(s["inproj_mm"], DC * b)
                        copy(ctxT[:, m, :], ps[:, 4 + m, :], s["ctxT_ready"])
                elif kind == "inproj":
                    act.wait_ge(s["inproj_mm"], DC * b + c + 1)
                    if b >= 1:
                        act.wait_ge(s["conv_done"], DC * (b - 1) + c + 1)
                    copy(xpad[:, c, TAPS - 1:XP], ps[:, 4 + c % 2, :], s["xpad_ready"])
                elif kind == "silu":
                    if b >= 1:
                        act.wait_ge(s["dt_ready"], b)
                    for k in range(DC):
                        act.wait_ge(s["conv_done"], DC * b + k + 1)
                        nc.scalar.activation(bt1[:, k, :], u[:, k, :], ACT.Tanh).then_inc(s["tanh_ready"], 1)
                elif kind == "xdbl":
                    act.wait_ge(s["xdbl_mm"], b + 1)
                    if b >= 1:
                        act.wait_ge(s["dt_mm"], DC * b)
                        act.wait_ge(s["bc_st"], 16 * b)
                    copy(xdbl[:], ps[0:DR + 2 * NS, 4, :], s["xdbl_ready"])
                elif kind == "softplus":
                    act.wait_ge(s["xm_ready"], b + 1)
                    act.wait_ge(s["u_ready"], DC * (b + 1))
                    nc.scalar.activation(bt1[:], dtu[b % 2], ACT.Exp).then_inc(s["e_ready"], 1)
                    act.wait_ge(s["ser_ready"], b + 1)
                    nc.scalar.activation(bt1[:], bt1[:], ACT.Ln, bias=1.0).then_inc(s["l_ready"], 1)
                elif kind == "step":
                    q = b * STEPS + c
                    g, k = divmod(c, DC)
                    act.wait_ge(s["dt_ready"], b + 1)
                    if q == 0:
                        act.wait_ge(s["const_set"], 4)
                    if q >= 2:
                        act.wait_ge(s["scan_done"], q - 1)
                    for n in range(NB):
                        a = nc.scalar.activation(dA[q % 2][:, n, 1:L], dt[b % 2][:, k, 1:L], ACT.Exp,
                                                 scale=An[:, k, NB * g + n:NB * g + n + 1])
                    a.then_inc(s["dA_done"], 1)
                elif kind == "gate":
                    for t in range(LT):
                        act.wait_ge(s["zin_ready"], LT * b + t + 1)
                        if t % 2 in used:
                            act.wait_ge(*used[t % 2])
                        nc.scalar.activation(tg[t % 2][:], zx[:, t, :], ACT.Tanh).then_inc(s["gth_ready"], 1)
                        used[t % 2] = (s["zg_ready"], LT * b + t + 1)
                    for t in range(LT):
                        act.wait_ge(s["zT_mm"], LT * b + t + 1)
                        if b >= 1:
                            act.wait_ge(s["yz_done"], LT * b)
                        copy(zT[:, t, :], ps[:, 4 + t % 2, :], s["zT_ready"])
                elif kind == "xnT":
                    for k in range(HC):
                        act.wait_ge(s["xnT_mm"], HC * b + k + 1)
                        if b >= 1:
                            act.wait_ge(s["gu_mm"], NI * b)
                            act.wait_ge(s["lg_mm"], LT * b)
                        copy(xnT[:, k, :], ps[:, 4 + k % 2, :], s["xnT_ready"])
                elif kind == "router":
                    n = LT * b + c
                    act.wait_ge(s["lg_mm"], n + 1)
                    if n >= 1:
                        act.wait_ge(s["slot_ready"], n)
                    copy(lg[:], ps[:, 4, 0:E], s["lg_ready"])
                    act.wait_ge(s["m_ready"], n + 1)
                    act.wait_ge(s["lg_ready"], n + 1)
                    nc.scalar.activation(ohp[:, 0, :], lg[:], ACT.Exp, bias=negm[:], accum_out=ssum[:])
                    nc.scalar.activation(e6[:], m8[:, 0:K], ACT.Exp, bias=negm[:]).then_inc(s["ex_ready"], 1)
                elif kind == "shared":
                    m = ISC[c]
                    act.wait_ge(s["gu_mm"], NI * b + c + 1)
                    if c % 2 in used:
                        act.wait_ge(*used[c % 2])
                    nc.scalar.activation(tg[c % 2][0:m, :], ps[0:m, 6, :], ACT.Tanh, scale=0.5)\
                        .then_inc(s["sth_ready"], 1)
                    used[c % 2] = (s["hs_ready"], NI * b + c + 1)

            def evac_tokens(i, j, first=False):
                act.wait_ge(s["xgT_mm"], 2 * i + j + 1)
                if not first:
                    act.wait_ge(s["egu_mm"], 2 * i + j - 1)
                copy(xgT[j], ps[:, 0, :].rearrange("p (c t) -> p c t", c=HC), s["xgT_ready"])

            def silu(i, j, first=False):
                act.wait_ge(s["egu_mm"], 2 * i + j + 1)
                if not first:
                    act.wait_ge(s["hT_mm"], 2 * i + j - 1)
                nc.scalar.activation(hh[j][:, 0:I], ps[:, 2 + j, 0:I], ACT.Silu).then_inc(s["silu_ready"], 1)

            def evac_acts(i, j, first=False):
                act.wait_ge(s["hT_mm"], 2 * i + j + 1)
                if not first:
                    act.wait_ge(s["y_mm"], 2 * i + j - 1)
                copy(hT[j], ps[:, 1, 0:IC * P].rearrange("p (c t) -> p c t", c=IC), s["hT_ready"])

            evac_tokens(0, 0, True)
            evac_tokens(0, 1, True)
            silu(0, 0, True)
            evac_acts(0, 0, True)
            evac_tokens(1, 0)
            silu(0, 1, True)
            evac_acts(0, 1, True)
            with act.Fori(1, NPAIR // 2 - 1) as i:
                evac_tokens(i, 1)
                silu(i, 0)
                evac_acts(i, 0)
                evac_tokens(i + 1, 0)
                silu(i, 1)
                evac_acts(i, 1)
            i = NPAIR // 2 - 1
            evac_tokens(i, 1)
            silu(i, 0)
            evac_acts(i, 0)
            silu(i, 1)
            evac_acts(i, 1)

        @block.vector
        def _(dve):
            count = [0]

            def link(ins):
                count[0] += 1
                ins.then_inc(s["dve"], 1)
                dve.wait_ge(s["dve"], count[0])

            V = nc.vector

            def norm(rows, n, half):
                for t in range(LT):
                    link(V.bn_stats(stats[:, t, :], rows[:, t, :]))
                    link(V.bn_aggr(mv[:, t, :], stats[:, t, :]))
                V.tensor_scalar(gsc[:, :, 0], mv[:, :, 1], EPS, None, ALU.add).then_inc(s["var_ready"], 1)
                dve.wait_ge(s["rstd_ready"], n + 1)
                if half:
                    link(V.tensor_scalar(gsc[:, :, 0], gsc[:, :, 0], 0.5, None, ALU.mult))
                link(V.scalar_tensor_tensor(gsc[:, :, 1], mv[:, :, 0], -1.0, gsc[:, :, 0], ALU.mult, ALU.mult))

            link(V.memset(zeros, 0.0))
            link(V.memset(csum[:], 0.0))
            for a in dA:
                link(V.memset(a[:, :, 0:1], 0.0))
            link(V.memset(xpad[:, :, 0:TAPS - 1], 0.0))
            dve.wait_ge(s["par_in"], 16 * 9)
            link(V.tensor_scalar(cw[:], cw[:], 0.5, None, ALU.mult))
            dve.wait_ge(s["pre_ev"], 6)
            link(V.tensor_scalar(vec[:, 0:DC], vec[:, 0:DC], 0.5, None, ALU.mult))
            dve.wait_ge(s["a_exp"], 1)
            V.tensor_scalar(An[:], An[:], -1.0, None, ALU.mult).then_inc(s["const_set"], 1)

            def scan(q, b, c):
                dve.wait_ge(s["dA_done"], q + 1)
                dve.wait_ge(s["dbu_done"], q + 1)
                V.tensor_tensor_scan(S[q % 3].rearrange("p n l -> p (n l)"), dA[q % 2].rearrange("p n l -> p (n l)"),
                                     S[q % 3].rearrange("p n l -> p (n l)"), 0.0, ALU.mult, ALU.add)\
                    .then_inc(s["scan_done"], 1)

            def weigh(q):
                n = q // DC
                dve.wait_ge(s["scan_done"], q + 1)
                dve.wait_ge(rep_in[n % 2], 32 * (n // 2 + 1))
                V.tensor_tensor(S[q % 3], S[q % 3], Crep[n % 2], ALU.mult).then_inc(s["cs_done"], 1)

            pending = []
            for kind, b, c in SCHEDULE:
                p = b % 2
                if kind != "step" and pending:
                    weigh(pending.pop())
                if kind == "inproj":
                    a = u[:, c, :]
                    dve.wait_ge(s["xpad_ready"], DC * b + c + 1)
                    if b >= 1:
                        dve.wait_ge(s["xdbl_mm"], b)
                    link(V.tensor_scalar(a, xpad[:, c, TAPS - 1:XP], cw[:, c, TAPS - 1:TAPS], vec[:, c:c + 1],
                                         ALU.mult, ALU.add))
                    for k in range(TAPS - 1):
                        ins = V.scalar_tensor_tensor(a, xpad[:, c, k:k + L], cw[:, c, k:k + 1], a,
                                                     ALU.mult, ALU.add)
                        if k < TAPS - 2:
                            link(ins)
                    ins.then_inc(s["conv_done"], 1)
                elif kind == "silu":
                    for k in range(DC):
                        dve.wait_ge(s["tanh_ready"], DC * b + k + 1)
                        V.scalar_tensor_tensor(u[:, k, :], bt1[:, k, :], 1.0, u[:, k, :], ALU.add, ALU.mult)\
                            .then_inc(s["u_ready"], 1)
                elif kind == "dt":
                    dve.wait_ge(s["dt_mm"], DC * b + c + 1)
                    if b >= 2:
                        dve.wait_ge(s["dA_done"], STEPS * (b - 1))
                    V.tensor_scalar(dt[p][:, c, :], ps[:, 5 - c % 2, :], vec[:, DC + c:DC + c + 1], None, ALU.add)\
                        .then_inc(s["xs_done"], 1)
                elif kind == "softplus":
                    dve.wait_ge(s["xs_done"], DC * (b + 1))
                    if b >= 2:
                        dve.wait_ge(s["dbu_done"], STEPS * (b - 1))
                    V.tensor_scalar(dtu[p], dt[p], 40.0, None, ALU.min).then_inc(s["xm_ready"], 1)
                    dve.wait_ge(s["l_ready"], b + 1)
                    link(V.copy_predicated(bt1[:], bt2[:].bitcast(U32), dtu[p]))
                    V.tensor_tensor(dt[p], dt[p], bt1[:], ALU.max).then_inc(s["dt_ready"], 1)
                    dve.wait_ge(s["dt_ready"], b + 1)
                    V.tensor_tensor(dtu[p], dt[p], u, ALU.mult).then_inc(s["dve"], 1)
                    count[0] += 1
                    for k in range(DC):
                        V.tensor_scalar(bt2[:, k, :], u[:, k, :], vec[:, 2 * DC + k:2 * DC + k + 1], None, ALU.mult)\
                            .then_inc(s["du_ready"], 1)
                elif kind == "step":
                    q = b * STEPS + c
                    scan(q, b, c)
                    if pending:
                        weigh(pending.pop())
                    pending.append(q)
                elif kind == "gate":
                    dve.wait_ge(x_in[p], 16 * (b // 2 + 1))
                    if b >= 1:
                        dve.wait_ge(s["xnT_mm"], HC * b)
                        dve.wait_ge(s["xn_st"], 16 * b)
                    norm(xb[p], 2 * b, True)
                    for t in range(LT):
                        V.tensor_scalar(zx[:, t, :], xb[p][:, t, :], gsc[:, t, 0:1], gsc[:, t, 1:2],
                                        ALU.mult, ALU.add).then_inc(s["zin_ready"], 1)
                    for t in range(LT):
                        dve.wait_ge(s["gth_ready"], LT * b + t + 1)
                        V.scalar_tensor_tensor(zx[:, t, :], tg[t % 2][:], 1.0, zx[:, t, :], ALU.add, ALU.mult)\
                            .then_inc(s["zg_ready"], 1)
                elif kind == "tail":
                    dve.wait_ge(s["yT_done"], STEPS * (b + 1))
                    dve.wait_ge(s["zT_ready"], LT * (b + 1))
                    for t in range(LT):
                        V.tensor_tensor(zT[:, t, :], ps_y[:, t, :], zT[:, t, :], ALU.mult).then_inc(s["yz_done"], 1)
                    for t in range(LT):
                        dve.wait_ge(s["yz_done"], LT * b + t + 1)
                        link(V.tensor_tensor(xb[p][:, t, :], xb[p][:, t, :], zT[:, t, :], ALU.add))
                    norm(xb[p], 2 * b + 1, False)
                    for t in range(LT):
                        V.tensor_scalar(zx[:, t, :], xb[p][:, t, :], gsc[:, t, 0:1], gsc[:, t, 1:2],
                                        ALU.mult, ALU.add).then_inc(s["xn_ready"], 1)
                elif kind == "router":
                    n = LT * b + c
                    if n == 0:
                        dve.wait_ge(s["iota_set"], 1)
                    dve.wait_ge(s["lg_ready"], n + 1)
                    link(V.max(m8[:], lg[:]))
                    V.tensor_scalar(negm[:], m8[:, 0:1], -1.0, None, ALU.mult).then_inc(s["m_ready"], 1)
                    link(V.max_index(i8[:], m8[:], lg[:]))
                    link(V.tensor_copy(i8f[:], i8[:, 0:K]))
                    link(V.tensor_tensor(oh[:], iota_e[:, None, :].to_broadcast([P, K, E]),
                                         i8f[:, :, None].to_broadcast([P, K, E]), ALU.is_equal))
                    if n >= 1:
                        dve.wait_ge(s["pos_mm"], n)
                        link(V.tensor_tensor(csum[:], csum[:], mask[:], ALU.add))
                    with nc.allow_low_precision("sums of one-hot rows, exact"):
                        V.tensor_reduce(mask[:], oh[:].rearrange("p k e -> p e k"), AX_X, ALU.add)\
                            .then_inc(s["mask_ready"], 1)
                    dve.wait_ge(s["ex_ready"], n + 1)
                    link(V.reciprocal(ssum[:], ssum[:]))
                    link(V.tensor_scalar(rec[:, n, :, 1], e6[:], ssum[:], None, ALU.mult))
                    V.tensor_copy(rec[:, n, :, 0], tokid[:, n:n + 1].to_broadcast([P, K]))
                    dve.wait_ge(s["pos_mm"], n + 1)
                    link(V.tensor_tensor(ohp[:], oh[:], ps[:, 5, None, 0:E].to_broadcast([P, K, E]), ALU.mult))
                    link(V.tensor_reduce(posk[:], ohp[:], AX_X, ALU.add))
                    link(V.scalar_tensor_tensor(slotf[:], i8f[:], float(CAP), posk[:], ALU.mult, ALU.add))
                    link(V.tensor_scalar(over[:], posk[:], float(CAP), float(2 * E * CAP), ALU.is_ge, ALU.mult))
                    V.tensor_tensor(slotu[:, n, :], slotf[:], over[:], ALU.add).then_inc(s["slot_ready"], 1)
                elif kind == "shared":
                    m = ISC[c]
                    th = tg[c % 2][0:m, :]
                    dve.wait_ge(s["sth_ready"], NI * b + c + 1)
                    if b >= 1:
                        dve.wait_ge(s["dn_mm"], LT * b)
                    link(V.scalar_tensor_tensor(th, th, 1.0, ps[0:m, 6, :], ALU.add, ALU.mult))
                    V.scalar_tensor_tensor(hs[0:m, c, :], th, 0.5, ps[0:m, 7, :], ALU.mult, ALU.mult)\
                        .then_inc(s["hs_ready"], 1)
                elif kind == "down":
                    dve.wait_ge(s["dn_mm"], LT * b + c + 1)
                    V.tensor_tensor(xb[p][:, c, :], xb[p][:, c, :], ps[:, 6 + c % 2, :], ALU.add)\
                        .then_inc(s["ob_ready"], 1)

                if kind == "tail" and b == B - 1:
                    for j in range(2):
                        V.memset(wd[j][96:P, :, 2, :], 0.0).then_inc(s["pad_set"], 1)
                        V.memset(hh[j][:, I:IC * P], 0.0)

            dve.wait_ge(s["tab_mm"], 1)
            V.tensor_copy(ids[:, :, 0], ps[:, 4, 0:NPAIR]).then_inc(s["ids_ready"], 1)
            V.tensor_copy(wts[:], ps[:, 4, 64:64 + NPAIR]).then_inc(s["ids_ready"], 1)
            V.tensor_copy(ids[0:CAP, :, 1], ps[0:CAP, 4, 128:128 + NPAIR]).then_inc(s["ids_ready"], 1)
            V.tensor_copy(ids[0:CAP, :, 2], ps[0:CAP, 4, 192:192 + NPAIR]).then_inc(s["ids_ready"], 1)
            dve.wait_ge(s["ids_ready"], 4)

            def at_pair(t, i, j):
                if isinstance(i, int):
                    return t[:, 2 * i + j:2 * i + j + 1]
                return t[:, bass.ds(2 * i + j, 1)]

            def index(i, j, first=False):
                if not first:
                    dve.wait_ge(s["xgT_mm"], 2 * i + j - 1)
                V.tensor_copy(idxg[j][:], at_pair(ids[:, :, 0], i, j)).then_inc(s["idx_ready"], 1)

            def gated(i, j):
                dve.wait_ge(s["silu_ready"], 2 * i + j + 1)
                V.tensor_tensor(hh[j][:, 0:I], hh[j][:, 0:I], ps[:, 4 + j, 0:I], ALU.mult).then_inc(s["h_ready"], 1)

            def weighted(i, j, first=False):
                dve.wait_ge(s["y_mm"], 2 * i + j + 1)
                if not first:
                    dve.wait_ge(s["sc_odd"], 16 * (2 * i + j - 1))
                for e in range(2):
                    V.tensor_copy(idxs[j][:, e:e + 1], at_pair(ids[0:CAP, :, 1 + e], i, j))
                V.tensor_copy(wcol[j][:], at_pair(wts, i, j)).then_inc(s["w_ready"], 1)
                dve.wait_ge(s["w_ready"], 2 * i + j + 1)
                V.tensor_scalar(ys[j], ps[:, 6 + j, :], wcol[j][:], None, ALU.mult).then_inc(s["y_ready"], 1)

            index(0, 0, True)
            index(0, 1, True)
            index(1, 0)
            gated(0, 0)
            index(1, 1)
            gated(0, 1)
            weighted(0, 0, True)

            def two_pairs(i, first=False):
                index(i + 1, 0)
                gated(i, 0)
                weighted(i - 1, 1, first)
                index(i + 1, 1)
                gated(i, 1)
                weighted(i, 0)

            two_pairs(1, True)
            with dve.Fori(2, NPAIR // 2 - 1) as i:
                two_pairs(i)
            i = NPAIR // 2 - 1
            gated(i, 0)
            weighted(i - 1, 1)
            gated(i, 1)
            weighted(i, 0)
            weighted(i, 1)

        @block.gpsimd
        def _(pool):
            G = nc.gpsimd
            G.iota(initrow[:, :, 0], pattern=[[1, CAP]], base=TRASH, channel_multiplier=0,
                   allow_small_or_imprecise_dtypes=True)
            G.memset(initrow[:, :, 1], 0.0)
            pool.wait_ge(s["dve"], 1)
            G.memset(ones[:], 1.0).then_inc(s["const_set"], 1)
            G.memset(ident[:], 0.0)
            G.memset(ltri[:], 1.0).then_inc(s["ser_chain"], 1)
            pool.wait_ge(s["ser_chain"], 1)
            G.affine_select(out=ident[:], in_=ident[:], compare_op=ALU.not_equal, fill=1.0, base=0,
                            pattern=[[-1, P]], channel_multiplier=1).then_inc(s["const_set"], 1)
            G.affine_select(out=ltri[:], in_=ltri[:], compare_op=ALU.is_gt, fill=0.0, base=0,
                            pattern=[[1, P]], channel_multiplier=-1).then_inc(s["const_set"], 1)
            G.memset(mhalf[:], -0.5)
            G.iota(iota_e[:], pattern=[[1, E]], base=0, channel_multiplier=0, allow_small_or_imprecise_dtypes=True)
            G.iota(tokid[:], pattern=[[P, B * LT]], base=0, channel_multiplier=1,
                   allow_small_or_imprecise_dtypes=True).then_inc(s["iota_set"], 1)
            chain = [1]

            def link(ins):
                chain[0] += 1
                ins.then_inc(s["ser_chain"], 1)
                pool.wait_ge(s["ser_chain"], chain[0])

            for kind, b, c in SCHEDULE:
                p = b % 2
                if kind in ("gate", "tail"):
                    pool.wait_ge(s["var_ready"], 2 * b + 1 + (kind == "tail"))
                    G.tensor_tensor(gsc[:, :, 0], gsc[:, :, 0], mhalf[:], ALU.pow).then_inc(s["rstd_ready"], 1)
                elif kind == "softplus":
                    pool.wait_ge(s["e_ready"], b + 1)
                    if b == 0:
                        pool.wait_ge(s["init_in"], 16 * 3)
                    else:
                        pool.wait_ge(s["duT_done"], b)
                    link(G.tensor_scalar(bt2[:], bt1[:], SERIES_BELOW, None, ALU.min))
                    link(G.tensor_scalar(dtu[p], bt2[:], -0.25, 1.0 / 3.0, ALU.mult, ALU.add))
                    link(G.tensor_tensor(dtu[p], dtu[p], bt2[:], ALU.mult))
                    link(G.tensor_scalar(dtu[p], dtu[p], -0.5, None, ALU.add))
                    link(G.tensor_tensor(dtu[p], dtu[p], bt2[:], ALU.mult))
                    link(G.tensor_scalar(dtu[p], dtu[p], 1.0, None, ALU.add))
                    link(G.tensor_tensor(dtu[p], dtu[p], bt2[:], ALU.mult))
                    G.tensor_scalar(bt2[:], bt1[:], SERIES_BELOW, None, ALU.is_lt).then_inc(s["ser_ready"], 1)
                elif kind == "step":
                    q = b * STEPS + c
                    n, k = divmod(q, DC)
                    pool.wait_ge(s["du_ready"], DC * (b + 1))
                    pool.wait_ge(rep_in[n % 2], 32 * (n // 2 + 1))
                    if q >= 3:
                        pool.wait_ge(s["yT_done"], q - 2)
                    G.tensor_tensor(S[q % 3], dtu[p][:, k, None, :].to_broadcast([P, NB, L]), Brep[n % 2], ALU.mult)\
                        .then_inc(s["dbu_done"], 1)
                elif kind == "router":
                    n = LT * b + c
                    if n == 0:
                        pool.wait_ge(s["init_in"], 16 * 3)
                    pool.wait_ge(s["slot_ready"], n + 1)
                    for k in range(K):
                        G.indirect_dma_start(
                            out=slot_dram, out_offset=bass.IndirectOffsetOnAxis(ap=slotu[:, n, k:k + 1], axis=0),
                            in_=rec[:, n, k, :], in_offset=None, bounds_check=E * CAP - 1, oob_is_err=False)\
                            .then_inc(s["scattered"], 16)

            pool.wait_ge(s["xn_st"], 16 * B)
            pool.wait_ge(s["out_st"], 16 * B)

            def hold():
                pool.sem_inc(s["held"], 1)

            def gather(i, j, first=False):
                pool.wait_ge(s["idx_ready"], 2 * i + j + 1)
                if not first:
                    pool.wait_ge(s["xgT_mm"], 2 * i + j - 1)
                hold()
                G.indirect_dma_start(out=xg[j], out_offset=None, in_=xn_dram,
                                     in_offset=bass.IndirectOffsetOnAxis(ap=idxg[j][:], axis=0),
                                     bounds_check=T + CAP - 1, oob_is_err=True).then_inc(xg_in[j], 16)

            def scatter(i, j, first=False):
                pool.wait_ge(s["y_ready"], 2 * i + j + 1)
                if not first:
                    pool.wait_ge(s["sc_odd"], 16 * (2 * i + j))
                for e, done in ((0, s["sc_even"]), (1, s["sc_odd"])):
                    if e == 1:
                        pool.wait_ge(s["sc_even"], 16 * (2 * i + j + 1))
                    hold()
                    G.indirect_dma_start(out=out, out_offset=bass.IndirectOffsetOnAxis(
                        ap=idxs[j][:, e:e + 1], axis=0), in_=ys[j][64 * e:64 * e + 64, :], in_offset=None,
                        bounds_check=T + CAP - 1, oob_is_err=True, compute_op=ALU.add).then_inc(done, 16)

            gather(0, 0, True)
            gather(0, 1, True)
            gather(1, 0)
            scatter(0, 0, True)
            gather(1, 1)
            scatter(0, 1)
            with pool.Fori(1, NPAIR // 2 - 1) as i:
                gather(i + 1, 0)
                scatter(i, 0)
                gather(i + 1, 1)
                scatter(i, 1)
            for j in range(2):
                scatter(NPAIR // 2 - 1, j)


_INS = ['x', 'ctx_1024', 'L0_xattn_in_proj_w', 'L0_xattn_conv_w', 'L0_xattn_conv_b', 'L0_xattn_x_proj_w',
        'L0_xattn_dt_proj_w', 'L0_xattn_dt_proj_b', 'L0_xattn_A_log', 'L0_xattn_D', 'L0_ffn_gate_w',
        'L0_ffn_w_gate', 'L0_ffn_w_up', 'L0_ffn_w_down', 'L0_ffn_sw_gate', 'L0_ffn_sw_up', 'L0_ffn_sw_down']


def kernel(**inputs):
    import numpy as np
    import concourse.bacc as bacc
    from concourse.bass_utils import run_bass_kernel_spmd

    nc = bacc.Bacc("TRN2", target_bir_lowering=False, num_devices=1, dynamic_dma_scratch_size=8192)
    arrays, args = {}, []
    for name in _INS:
        a = np.ascontiguousarray(inputs[name])
        arrays[f"in_{name}"] = a
        args.append(nc.dram_tensor(f"in_{name}", a.shape, mybir.dt.from_np(a.dtype), kind="ExternalInput").ap())
    out = nc.dram_tensor("out_rows", [T + CAP, H], F32, kind="ExternalOutput").ap()
    build(nc, *args, out)
    r = run_bass_kernel_spmd(nc, [arrays], core_ids=[0])
    return r.results[0]["out_rows"][:T].reshape(B, L, H)
```

```python
from contextlib import ExitStack

import concourse.bass as bass
from concourse import mybir

F32 = mybir.dt.float32
BF16 = mybir.dt.bfloat16
U32 = mybir.dt.uint32
ALU = mybir.AluOpType
ACT = mybir.ActivationFunctionType
AX_X = mybir.AxisListType.X

P = 128
B, L, H = 4, 512, 512
DM, DI, NS, DR = 256, 512, 16, 16
TAPS = 4
E, K, I, CAP = 64, 6, 352, 64
IS = 704
T = B * L
EPS = 1e-5
DC = DI // P
LT = L // P
HC = H // P
NB = 2
NG = NS // NB
STEPS = NG * DC
ISC = [P] * (IS // P) + [IS % P]
NI = len(ISC)
NPAIR = E // 2
IC = 3
IREST = I - 2 * P
TRASH = T
SERIES_BELOW = 0.03


def build(nc, x, ctx_1024, in_proj_w, conv_w, conv_b, x_proj_w, dt_proj_w, dt_proj_b, A_log, D,
          gate_w, w_gate, w_up, w_down, sw_gate, sw_up, sw_down, out):
    bc_dram = nc.dram_tensor("bc_rows", [B, 2 * NS, L], F32, kind="Internal").ap()
    xn_dram = nc.dram_tensor("xn_rows", [T + CAP, H], F32, kind="Internal").ap()
    slot_dram = nc.dram_tensor("slot_table", [E * CAP, 2], F32, kind="Internal").ap()

    with ExitStack() as ctx:
        ctx.enter_context(nc.allow_non_contiguous_dma(reason="small parameter loads"))

        def sb(name, shape, dt=F32):
            return ctx.enter_context(nc.sbuf_tensor(name, shape, dt))

        def sem(name):
            return ctx.enter_context(nc.semaphore(name))

        GW = 2 * HC * I
        DWN = 2 * IC * H
        PAIRW = 2 * GW + DWN
        arena = sb("arena", [P, 2 * PAIRW])
        at = [0]

        def carve(t, words):
            a = t[:, at[0]:at[0] + words]
            at[0] += words
            return a

        dA = [carve(arena, NB * L).rearrange("p (n l) -> p n l", n=NB) for _ in range(2)]
        S = [carve(arena, NB * L).rearrange("p (n l) -> p n l", n=NB) for _ in range(3)]
        S.append(sb("S3", [P, NB, L])[:])
        Brep = [carve(arena, NB * L).rearrange("p (n l) -> p n l", n=NB) for _ in range(2)]
        Crep = [carve(arena, NB * L).rearrange("p (n l) -> p n l", n=NB) for _ in range(2)]
        dt = [carve(arena, DC * L).rearrange("p (c l) -> p c l", c=DC) for _ in range(2)]
        dtu = [carve(arena, DC * L).rearrange("p (c l) -> p c l", c=DC) for _ in range(2)]
        assert at[0] <= 2 * PAIRW
        at[0] = 0
        wg, wu, wd = [], [], []
        for j in range(2):
            wg.append(carve(arena, GW).rearrange("p (e c i) -> p e c i", e=2, c=HC))
            wu.append(carve(arena, GW).rearrange("p (e c i) -> p e c i", e=2, c=HC))
            wd.append(carve(arena, DWN).rearrange("p (e c h) -> p e c h", e=2, c=IC))

        XP = L + TAPS - 1
        prep = sb("prep", [P, DC * L + DC * XP + LT * DM + 2 * L])
        at[0] = 0
        u = carve(prep, DC * L).rearrange("p (c l) -> p c l", c=DC)
        xpad = carve(prep, DC * XP).rearrange("p (c l) -> p c l", c=DC)
        cin = carve(prep, LT * DM).rearrange("p (t d) -> p t d", t=LT)
        ctxT = carve(prep, 2 * L).rearrange("p (m l) -> p m l", m=2)
        at[0] = 0
        xg, xgT, hh, hT, ys = [], [], [], [], []
        for j in range(2):
            xg.append(carve(prep, H))
            xgT.append(carve(prep, H).rearrange("p (c t) -> p c t", c=HC))
            hh.append(carve(prep, IC * P))
            hT.append(carve(prep, IC * P).rearrange("p (c t) -> p c t", c=IC))
            ys.append(carve(prep, H))
        tab = carve(prep, 2 * P)[0:NPAIR]
        ids = carve(prep, 3 * NPAIR).bitcast(U32).rearrange("p (q k) -> p q k", k=3)
        wts = carve(prep, NPAIR)

        xb = [sb(f"xb{j}", [P, LT, H]) for j in range(2)]
        zx = sb("zx", [P, LT, H])
        zT = sb("zT", [P, LT, DI])
        xnT = sb("xnT", [P, HC, L])
        hs = sb("hs", [P, NI, L])
        swg = sb("swg", [P, HC, IS])
        swu = sb("swu", [P, HC, IS])
        swd = sb("swd", [P, NI, H])
        bt1 = sb("bt1", [P, DC, L])
        bt2 = sb("bt2", [P, DC, L])
        tg = [sb(f"tg{j}", [P, L]) for j in range(2)]
        winT = sb("winT", [P, 2, DI])
        xpT = sb("xpT", [P, DC, DR + 2 * NS])
        dtwT = sb("dtwT", [DR, DI])
        xdbl = sb("xdbl", [DR + 2 * NS, L])
        gwT = sb("gwT", [P, HC, E])
        ident = sb("ident", [P, P])
        ltri = sb("ltri", [P, P], BF16)
        ones = sb("ones", [P, P], BF16)
        vec = sb("vec", [P, 3 * DC])
        cw = sb("cw", [P, DC, TAPS])
        An = sb("An", [P, DC, NS])
        stats = sb("stats", [P, LT, 6])
        mv = sb("mv", [P, LT, 2])
        gsc = sb("gsc", [P, LT, 2])
        mhalf = sb("mhalf", [P, LT])
        iota_e = sb("iota_e", [P, E])
        tokid = sb("tokid", [P, B * LT])
        csum = sb("csum", [P, E], BF16)
        mask = sb("mask", [P, E], BF16)
        lg = sb("lg", [P, E])
        m8 = sb("m8", [P, 8])
        i8 = sb("i8", [P, 8], U32)
        i8f = sb("i8f", [P, K])
        negm = sb("negm", [P, 1])
        ssum = sb("ssum", [P, 1])
        e6 = sb("e6", [P, K])
        oh = sb("oh", [P, K, E])
        ohp = sb("ohp", [P, K, E])
        posk = sb("posk", [P, K])
        slotf = sb("slotf", [P, K])
        over = sb("over", [P, K])
        slotu = sb("slotu", [P, B * LT, K], U32)
        rec = sb("rec", [P, B * LT, K, 2])
        idxg = [sb(f"idxg{j}", [P, 1], U32) for j in range(2)]
        idxs = [sb(f"idxs{j}", [CAP, 2], U32) for j in range(2)]
        wcol = [sb(f"wcol{j}", [P, 1]) for j in range(2)]
        ps = ctx.enter_context(nc.psum_tensor("ps", [P, 8, 512], F32))
        ps_y = ps[:, 0:4, :]

        raw_win = zx[:, 0:2, :].rearrange("p t (c d) -> p (t c) d", d=DM)
        raw_gw = zT[0:E, 0, :]
        raw_xp = zT[0:DR + 2 * NS, 1, :]
        raw_dtw = zT[:, 2, 0:DC * DR].rearrange("p (c r) -> p c r", c=DC)
        raw_vec = zT[0:3 * DC, 3, 0:P]
        zeros = bt2[0:CAP, 0, :]
        initrow = bt2[0:E, 1, 0:2 * CAP].rearrange("e (c t) -> e c t", t=2)

        names = """par_in sw_in const_set a_exp iota_set init_in pre_t pre_ev
            ctx_in0 ctx_in1 x_in0 x_in1 bc_st rep_in0 rep_in1 xn_st out_st scattered
            ctxT_mm ctxT_ready inproj_mm xpad_ready conv_done tanh_ready u_ready xdbl_mm xdbl_ready
            dt_mm xs_done xm_ready e_ready ser_chain ser_ready l_ready dt_ready dtu_ready du_ready duT_done
            dA_done dbu_done scan_done cs_done yT_done
            var_ready rstd_ready gsc_ready gth_ready zg_ready zT_mm zT_ready yz_done xn_ready xnT_mm xnT_ready
            lg_mm lg_ready m_ready ex_ready mask_ready pos_mm slot_ready
            g_mm gu_mm sth_ready sa_ready hs_ready dn_mm ob_ready dve
            held tab_in tab_mm ids_ready idx_ready w_ready xg_in0 xg_in1 xgT_mm xgT_ready
            gu_in0 gu_in1 wd_in0 wd_in1 egu_mm silu_ready h_ready hT_mm hT_ready y_mm y_ready
            sc_even sc_odd pad_set""".split()
        s = {n: sem(n) for n in names}
        rep_in = [s["rep_in0"], s["rep_in1"]]
        x_in = [s["x_in0"], s["x_in1"]]
        xg_in = [s["xg_in0"], s["xg_in1"]]
        gu_in = [s["gu_in0"], s["gu_in1"]]
        wd_in = [s["wd_in0"], s["wd_in1"]]

        def first_phase():
            parts = []

            def add(time, engine, kind, b, c=None):
                parts.append((time, len(parts), engine, kind, b, c))

            for q in range(B * STEPS):
                b, step = divmod(q, STEPS)
                add(q - 1.4, "pool", "dbu", b, step)
                add(q - 1.0, "act", "dA", b, step)
                add(q, "dve", "scan", b, step)
                add(q + 1.05, "dve", "weigh", b, step)
                add(q + 1.5, "pe", "yT", b, step)
                if step % DC == DC - 1 and gi(b, step // DC) + 2 < B * NG:
                    add(q + 1.6, "sp", "rep", b, step)
            for b in range(B):
                t = STEPS * (b - 1) + 10 if b else -20
                if b:
                    add(t - 4, "sp", "ctx_load", b)
                add(t, "pe", "ctx", b)
                add(t + 0.4, "act", "ctx", b)
                for c in range(DC):
                    mm = t + 1.6 + 2 * (c // 2)
                    add(mm, "pe", "inproj", b, c)
                    add(mm + 0.4, "act", "xpad", b, c)
                    add(t + 2.5 + c, "dve", "conv", b, c)
                    add(t + 2.8 + c, "act", "tanh", b, c)
                    add(t + 3.2 + c, "dve", "u", b, c)
                    add(t + 7.8 + 0.8 * (c // 2), "pe", "dt", b, c)
                    add(t + 8.2 + 0.8 * (c // 2), "act", "xs", b, c)
                    add(t + 9.6 + 1.7 * c, "pool", "series", b, c)
                add(t + 7, "pe", "xdbl", b)
                add(t + 7.3, "act", "xdbl", b)
                add(t + 7.4, "sp", "xdbl", b)
                add(t + 9.2, "dve", "xm", b)
                add(t + 9.3, "act", "exp", b)
                add(t + 16.5, "act", "ln", b)
                add(t + 16.8, "dve", "softplus", b)
                for c in range(DC):
                    add(t + 18.2 + 0.2 * c, "act", "du", b, c)
                t = STEPS * b
                for c in range(LT):
                    add(t + 8 + c, "dve", "gate_stats", b, c)
                    add(t + 13 + c, "act", "gate", b, c)
                    add(t + 13.5 + c, "dve", "gate", b, c)
                    add(t + 20.4 + 0.5 * (c // 2), "pe", "gate", b, c)
                    add(t + 20.8 + 0.5 * (c // 2), "act", "zT", b, c)
                add(t + 12.2, "dve", "gate_var", b)
                add(t + 12.3, "pool", "gate_rstd", b)
                add(t + 12.6, "dve", "gate_scale", b)
                add(t + 0.7, "pe", "duT", b)
                t = STEPS * (b + 1)
                add(t + 0.6, "dve", "yz", b)
                for c in range(LT):
                    add(t + 1.2 + 0.4 * c, "dve", "x2", b, c)
                    add(t + 3.3 + 0.3 * c, "act", "xn", b, c)
                add(t + 2.7, "dve", "var", b)
                add(t + 2.8, "pool", "rstd", b)
                add(t + 3.1, "dve", "scale", b)
                add(t + 4.6, "sp", "xn", b)
                for c in range(HC):
                    add(t + 5 + c // 2, "pe", "xnT", b, c)
                    add(t + 5.4 + c // 2, "act", "xnT", b, c)
                for c in range(LT):
                    n = t + 7 + 2 * c
                    add(n, "pe", "logits", b, c)
                    add(n + 0.3, "act", "logits", b, c)
                    add(n + 0.6, "dve", "choose", b, c)
                    add(n + 0.9, "act", "weights", b, c)
                    add(n + 1.6, "pe", "pos", b, c)
                    add(n + 2.0, "dve", "slots", b, c)
                    add(n + 2.7, "pool", "scatter", b, c)
                unit = 0
                for c in range(NI):
                    for k in range(4):
                        add(t + 7.1 + 0.66 * unit, "pe", "shared", b, (c, k))
                        unit += 1
                    add(t + 7.1 + 0.66 * unit - 1.2, "act", "shared", b, c)
                    add(t + 7.1 + 0.66 * unit - 0.4, "dve", "shared", b, c)
                for c in range(LT):
                    for k in range(NI // 2):
                        add(t + 7.1 + 0.66 * unit, "pe", "down", b, (c, k))
                        unit += 1
                    add(t + 7.1 + 0.66 * unit - 0.3, "dve", "down", b, c)
                add(t + 31.5, "sp", "out", b)
            add(STEPS * B + 2, "dve", "pads", B - 1)
            add(STEPS * B + 2.1, "sp", "weights", B - 1)
            parts.sort()
            return parts

        def gi(b, g):
            return b * NG + g

        PARTS = first_phase()

        def mine(engine):
            return [(kind, b, c) for _, _, e, kind, b, c in PARTS if e == engine]

        def gate_up(sp, q, j):
            for w, dst in ((w_gate, wg), (w_up, wu)):
                src = w.rearrange("(q e) (p c) i -> q p e (c i)", e=2, c=HC)
                sp.dma_start(dst[j].rearrange("p e c i -> p e (c i)"), pick(src, q)).then_inc(gu_in[j], 16)

        def pick(a, q):
            return a[bass.ds(q, 1)].rearrange("o p e f -> (o p) e f") if not isinstance(q, int) else a[q]

        def down(sp, q, j):
            head = w_down[:, 0:2 * P, :].rearrange("(q e) (p c) h -> q p e (c h)", e=2, c=2)
            rest = w_down[:, 2 * P:I, :].rearrange("(q e) p h -> q p e h", e=2)
            sp.dma_start(wd[j][:, :, 0:2, :].rearrange("p e c h -> p e (c h)"), pick(head, q)).then_inc(wd_in[j], 16)
            sp.dma_start(wd[j][0:IREST, :, 2, :], pick(rest, q)).then_inc(wd_in[j], 16)

        def weights(sp, q, j):
            gate_up(sp, q, j)
            sp.wait_ge(s["pad_set"], 2)
            down(sp, q, j)

        block = ctx.enter_context(nc.Block())

        @block.sync
        def _(sp):
            def load(dst, src, sm):
                return sp.dma_start(dst, src).then_inc(sm, 16)

            load(cin, ctx_1024[0].rearrange("(t p) d -> p t d", p=P), s["ctx_in0"])
            load(raw_win, in_proj_w.rearrange("(c p) d -> p c d", p=P), s["par_in"])
            load(raw_xp, x_proj_w, s["par_in"])
            load(raw_dtw, dt_proj_w.rearrange("(c p) r -> p c r", p=P), s["par_in"])
            load(raw_vec[0:DC], conv_b.rearrange("(c p) -> c p", p=P), s["par_in"])
            load(raw_vec[DC:2 * DC], dt_proj_b.rearrange("(c p) -> c p", p=P), s["par_in"])
            load(raw_vec[2 * DC:3 * DC], D.rearrange("(c p) -> c p", p=P), s["par_in"])
            load(cw[:], conv_w.rearrange("(c p) o k -> p c (o k)", p=P), s["par_in"])
            load(An[:], A_log.rearrange("(c p) n -> p c n", p=P), s["par_in"])
            load(raw_gw, gate_w, s["par_in"])
            load(xb[0][:], x[0].rearrange("(t p) c -> p t c", p=P), x_in[0])
            sp.wait_ge(s["const_set"], 1)
            load(xn_dram[T:T + CAP, :], zeros, s["init_in"])
            load(out[T:T + CAP, :], zeros, s["init_in"])
            load(slot_dram.rearrange("(e c) t -> e (c t)", e=E),
                 initrow.rearrange("e c t -> e (c t)"), s["init_in"])
            load(swg[:], sw_gate.rearrange("(p c) i -> p c i", c=HC), s["sw_in"])
            load(swu[:], sw_up.rearrange("(p c) i -> p c i", c=HC), s["sw_in"])
            load(swd[:, 0:NI - 1, :], sw_down[0:(NI - 1) * P].rearrange("(c p) h -> p c h", p=P), s["sw_in"])
            load(swd[0:IS % P, NI - 1, :], sw_down[(NI - 1) * P:IS], s["sw_in"])

            def rep(b, g):
                n = gi(b, g)
                if g == 0:
                    sp.wait_ge(s["bc_st"], 16 * (b + 1))
                if n >= 2:
                    sp.wait_ge(s["dbu_done"], DC * (n - 1))
                    sp.wait_ge(s["cs_done"], DC * (n - 1))
                for dst, row in ((Brep, 0), (Crep, NS)):
                    src = bc_dram[b:b + 1, row + NB * g:row + NB * (g + 1), :].to_broadcast([P, NB, L])
                    load(dst[n % 2], src, rep_in[n % 2])

            load(xb[1][:], x[1].rearrange("(t p) c -> p t c", p=P), x_in[1])
            for kind, b, c in mine("sp"):
                if kind == "ctx_load":
                    sp.wait_ge(s["ctxT_mm"], 2 * b)
                    load(cin, ctx_1024[b].rearrange("(t p) d -> p t d", p=P), s["ctx_in0"])
                elif kind == "xdbl":
                    sp.wait_ge(s["xdbl_ready"], b + 1)
                    load(bc_dram[b], xdbl[DR:DR + 2 * NS, :], s["bc_st"])
                    if b == 0:
                        rep(0, 0)
                        rep(0, 1)
                elif kind == "rep":
                    n = gi(b, c // DC) + 2
                    rep(n // NG, n % NG)
                elif kind == "out":
                    sp.wait_ge(s["ob_ready"], LT * (b + 1))
                    load(out[b * L:(b + 1) * L].rearrange("(t p) c -> p t c", p=P), xb[b % 2][:], s["out_st"])
                    if b + 2 < B:
                        sp.wait_ge(s["out_st"], 16 * (b + 1))
                        load(xb[b % 2][:], x[b + 2].rearrange("(t p) c -> p t c", p=P), x_in[b % 2])
                elif kind == "xn":
                    sp.wait_ge(s["xn_ready"], LT * (b + 1))
                    load(xn_dram[b * L:(b + 1) * L].rearrange("(t p) c -> p t c", p=P), zx[:], s["xn_st"])
                elif kind == "weights":
                    sp.wait_ge(s["yT_done"], B * STEPS)
                    sp.wait_ge(s["dA_done"], B * STEPS)
                    for j in range(2):
                        weights(sp, j, j)
            sp.wait_ge(s["scattered"], 16 * B * LT * K)
            load(tab[:], slot_dram.rearrange("(q c) t -> q (c t)", q=NPAIR), s["tab_in"])

            def free_then_load(i, j):
                sp.wait_ge(s["egu_mm"], 2 * i + j - 1)
                gate_up(sp, 2 * i + j, j)
                sp.wait_ge(s["y_mm"], 2 * i + j - 1)
                down(sp, 2 * i + j, j)

            with sp.Fori(1, NPAIR // 2) as i:
                for j in range(2):
                    free_then_load(i, j)
            sp.wait_ge(s["sc_odd"], 16 * NPAIR)
            sp.wait_ge(s["sc_even"], 16 * NPAIR)
            sp.wait_ge(s["out_st"], 16 * B)
            sp.wait_ge(s["xn_st"], 16 * B)
            sp.wait_ge(s["init_in"], 16 * 3)

        @block.tensor
        def _(pe):
            freed = {}

            def claim(bank):
                if bank in freed:
                    pe.wait_ge(*freed[bank])

            def transpose(dst, src, **kw):
                k = src.shape[0]
                return nc.tensor.matmul(dst, src, ident[0:k, 0:k], is_transpose=True, **kw)

            def flip(bank, cols, srcs, **kw):
                for n, a in enumerate(srcs):
                    m, k = a.shape[1], a.shape[0]
                    last = transpose(ps[0:m, bank, cols + n * k:cols + (n + 1) * k], a, start=True, stop=True)
                return last

            pe.wait_ge(s["const_set"], 3)
            pe.wait_ge(s["par_in"], 16 * 9)
            for m in range(2):
                flip(4 + m, 0, [raw_win[:, c, m * P:(m + 1) * P] for c in range(DC)]).then_inc(s["pre_t"], 1)
            flip(6, 0, [raw_gw[:, c::HC] for c in range(HC)]).then_inc(s["pre_t"], 1)
            flip(7, 0, [raw_xp[:, c * P:(c + 1) * P] for c in range(DC)])
            flip(7, 256, [raw_vec]).then_inc(s["pre_t"], 1)
            pe.wait_ge(s["pre_ev"], 2)
            flip(4, 0, [raw_dtw[:, c, :] for c in range(DC)]).then_inc(s["pre_t"], 1)
            freed.update({4: (s["pre_ev"], 6), 5: (s["pre_ev"], 6), 6: (s["pre_ev"], 6), 7: (s["pre_ev"], 6)})
            pe.wait_ge(s["pre_ev"], 6)

            for kind, b, c in mine("pe"):
                if kind == "ctx":
                    pe.wait_ge(s["ctx_in0"], 16 * (b + 1))
                    for m in range(2):
                        claim(4 + m)
                        flip(4 + m, 0, [cin[:, t, m * P:(m + 1) * P] for t in range(LT)]).then_inc(s["ctxT_mm"], 1)
                        freed[4 + m] = (s["ctxT_ready"], 2 * b + m + 1)
                elif kind == "inproj":
                    bank = 4 + c % 2
                    claim(bank)
                    pe.wait_ge(s["ctxT_ready"], 2 * b + 2)
                    for m in range(2):
                        mm = nc.tensor.matmul(ps[:, bank, :], winT[:, m, c * P:(c + 1) * P], ctxT[:, m, :],
                                              start=(m == 0), stop=(m == 1))
                    mm.then_inc(s["inproj_mm"], 1)
                    freed[bank] = (s["xpad_ready"], DC * b + c + 1)
                elif kind == "xdbl":
                    claim(4)
                    pe.wait_ge(s["u_ready"], DC * (b + 1))
                    for k in range(DC):
                        mm = nc.tensor.matmul(ps[0:DR + 2 * NS, 4, :], xpT[:, k, :], u[:, k, :],
                                              start=(k == 0), stop=(k == DC - 1))
                    mm.then_inc(s["xdbl_mm"], 1)
                    freed[4] = (s["xdbl_ready"], b + 1)
                elif kind == "dt":
                    bank = 5 - c % 2
                    claim(bank)
                    pe.wait_ge(s["xdbl_ready"], b + 1)
                    nc.tensor.matmul(ps[:, bank, :], dtwT[:, c * P:(c + 1) * P], xdbl[0:DR, :],
                                     start=True, stop=True).then_inc(s["dt_mm"], 1)
                    freed[bank] = (s["xs_done"], DC * b + c + 1)
                elif kind == "duT":
                    pe.wait_ge(s["du_ready"], DC * (b + 1))
                    for t in range(LT):
                        if b >= 1:
                            pe.wait_ge(s["yz_done"], LT * (b - 1) + t + 1)
                        for k in range(DC):
                            mm = transpose(ps_y[:, t, k * P:(k + 1) * P], bt2[:, k, t * P:(t + 1) * P],
                                           start=(k == 0), stop=False, skip_group_check=True)
                    mm.then_inc(s["duT_done"], 1)
                elif kind == "yT":
                    q = b * STEPS + c
                    k = c % DC
                    pe.wait_ge(s["cs_done"], q + 1)
                    for n in range(NB):
                        for t in range(LT):
                            mm = transpose(ps_y[:, t, k * P:(k + 1) * P], S[q % 4][:, n, t * P:(t + 1) * P],
                                           start=False, stop=(c >= STEPS - DC and n == NB - 1),
                                           skip_group_check=True)
                    mm.then_inc(s["yT_done"], 1)
                elif kind == "gate":
                    bank = 4 + c % 2
                    claim(bank)
                    pe.wait_ge(s["zg_ready"], LT * (b + 1))
                    flip(bank, 0, [zx[:, k, c * P:(c + 1) * P] for k in range(DC)]).then_inc(s["zT_mm"], 1)
                    freed[bank] = (s["zT_ready"], LT * b + c + 1)
                elif kind == "xnT":
                    pe.wait_ge(s["xn_ready"], LT * (b + 1))
                    bank = 4 + c % 2
                    claim(bank)
                    flip(bank, 0, [zx[:, t, c::HC] for t in range(LT)]).then_inc(s["xnT_mm"], 1)
                    freed[bank] = (s["xnT_ready"], HC * b + c + 1)
                elif kind == "logits":
                    pe.wait_ge(s["xnT_ready"], HC * (b + 1))
                    claim(4)
                    for k in range(HC):
                        mm = nc.tensor.matmul(ps[:, 4, 0:E], xnT[:, k, c * P:(c + 1) * P], gwT[:, k, :],
                                              start=(k == 0), stop=(k == HC - 1))
                    mm.then_inc(s["lg_mm"], 1)
                    freed[4] = (s["lg_ready"], LT * b + c + 1)
                elif kind == "pos":
                    claim(5)
                    pe.wait_ge(s["mask_ready"], LT * b + c + 1)
                    nc.tensor.matmul(ps[:, 5, 0:E], ltri[:], mask[:], start=True, stop=False)
                    nc.tensor.matmul(ps[:, 5, 0:E], ones[:], csum[:], start=False, stop=True).then_inc(s["pos_mm"], 1)
                    freed[5] = (s["slot_ready"], LT * b + c + 1)
                elif kind == "shared":
                    c, half = c
                    m = ISC[c]
                    if b == 0 and c == 0 and half == 0:
                        pe.wait_ge(s["sw_in"], 16 * 4)
                    bank, w = ((6, swg), (7, swu))[half // 2]
                    if half % 2 == 0:
                        pe.wait_ge(s["xnT_ready"], HC * (b + 1))
                        claim(bank)
                    for k in (0, 1) if half % 2 == 0 else (2, 3):
                        mm = nc.tensor.matmul(ps[0:m, bank, :], w[:, k, c * P:c * P + m], xnT[:, k, :],
                                              start=(k == 0), stop=(k == HC - 1))
                    if half % 2:
                        mm.then_inc(s["g_mm" if bank == 6 else "gu_mm"], 1)
                        freed[bank] = (s["hs_ready"], NI * b + c + 1)
                elif kind == "down":
                    c, third = c
                    bank = 6 + c % 2
                    if third == 0:
                        claim(bank)
                        pe.wait_ge(s["hs_ready"], NI * (b + 1))
                    for k in (2 * third, 2 * third + 1):
                        m = ISC[k]
                        mm = nc.tensor.matmul(ps[:, bank, :], hs[0:m, k, c * P:(c + 1) * P], swd[0:m, k, :],
                                              start=(k == 0), stop=(k == NI - 1))
                    if third == NI // 2 - 1:
                        mm.then_inc(s["dn_mm"], 1)
                        freed[bank] = (s["ob_ready"], LT * b + c + 1)

            pe.wait_ge(s["tab_in"], 16)
            claim(4)
            claim(5)
            flip(4, 0, [tab[:, 0::2]])
            flip(4, 64, [tab[:, 1::2]])
            flip(4, 128, [tab[:, 0:2 * CAP:2]])
            flip(4, 192, [tab[:, 2 * CAP:4 * CAP:2]]).then_inc(s["tab_mm"], 1)
            for bank in (6, 7):
                claim(bank)
            pe.wait_ge(s["ids_ready"], 4)
            pe.wait_ge(s["yz_done"], LT * B)

            def tokens(i, j, first=False):
                pe.wait_ge(xg_in[j], 16 * (i + 1))
                if not first:
                    pe.wait_ge(s["xgT_ready"], 2 * i + j)
                flip(0, 0, [xg[j][:, k::HC] for k in range(HC)]).then_inc(s["xgT_mm"], 1)

            def gate_up_mm(i, j, first=False):
                pe.wait_ge(s["xgT_ready"], 2 * i + j + 1)
                pe.wait_ge(gu_in[j], 32 * (i + 1))
                if not first:
                    pe.wait_ge(s["h_ready"], 2 * i + j - 1)
                for bank, w in ((2 + j, wg[j]), (4 + j, wu[j])):
                    for k in range(HC):
                        for e in range(2):
                            mm = nc.tensor.matmul(ps[64 * e:64 * e + 64, bank, 0:I],
                                                  xgT[j][:, k, 64 * e:64 * e + 64], w[:, e, k, :],
                                                  start=(k == 0), stop=(k == HC - 1))
                mm.then_inc(s["egu_mm"], 1)

            def acts(i, j, first=False):
                pe.wait_ge(s["h_ready"], 2 * i + j + 1)
                if not first:
                    pe.wait_ge(s["hT_ready"], 2 * i + j)
                flip(1, 0, [hh[j][:, 0:2 * P:2], hh[j][:, 1:2 * P:2], hh[j][:, 2 * P:3 * P]]).then_inc(s["hT_mm"], 1)

            def down_mm(i, j, first=False):
                pe.wait_ge(s["hT_ready"], 2 * i + j + 1)
                pe.wait_ge(wd_in[j], 32 * (i + 1))
                if not first:
                    pe.wait_ge(s["y_ready"], 2 * i + j - 1)
                for k in range(IC):
                    for e in range(2):
                        mm = nc.tensor.matmul(ps[64 * e:64 * e + 64, 6 + j, :], hT[j][:, k, 64 * e:64 * e + 64],
                                              wd[j][:, e, k, :], start=(k == 0), stop=(k == IC - 1))
                mm.then_inc(s["y_mm"], 1)

            tokens(0, 0, True)
            tokens(0, 1)
            gate_up_mm(0, 0, True)
            acts(0, 0, True)
            tokens(1, 0)
            gate_up_mm(0, 1, True)
            down_mm(0, 0, True)
            acts(0, 1)

            def two_pairs(i, first=False):
                tokens(i, 1)
                gate_up_mm(i, 0)
                down_mm(i - 1, 1, first)
                acts(i, 0)
                tokens(i + 1, 0)
                gate_up_mm(i, 1)
                down_mm(i, 0)
                acts(i, 1)

            two_pairs(1, True)
            with pe.Fori(2, NPAIR // 2 - 1) as i:
                two_pairs(i)
            i = NPAIR // 2 - 1
            tokens(i, 1)
            gate_up_mm(i, 0)
            down_mm(i - 1, 1)
            acts(i, 0)
            gate_up_mm(i, 1)
            down_mm(i, 0)
            acts(i, 1)
            down_mm(i, 1)

        @block.scalar
        def _(act):
            def copy(dst, src, sm):
                nc.scalar.copy(dst, src).then_inc(sm, 1)

            act.wait_ge(s["par_in"], 16 * 9)
            nc.scalar.activation(An[:], An[:], ACT.Exp).then_inc(s["a_exp"], 1)
            act.wait_ge(s["pre_t"], 2)
            for m in range(2):
                copy(winT[:, m, :], ps[:, 4 + m, :], s["pre_ev"])
            act.wait_ge(s["pre_t"], 3)
            copy(gwT[:], ps[:, 6, 0:HC * E].rearrange("p (c e) -> p c e", c=HC), s["pre_ev"])
            act.wait_ge(s["pre_t"], 4)
            w = DR + 2 * NS
            copy(xpT[:], ps[:, 7, 0:DC * w].rearrange("p (c r) -> p c r", c=DC), s["pre_ev"])
            copy(vec[:], ps[:, 7, 256:256 + 3 * DC], s["pre_ev"])
            act.wait_ge(s["pre_t"], 5)
            copy(dtwT[:], ps[0:DR, 4, :], s["pre_ev"])

            used = {}

            for kind, b, c in mine("act"):
                p = b % 2
                if kind == "ctx":
                    for m in range(2):
                        act.wait_ge(s["ctxT_mm"], 2 * b + m + 1)
                        if b >= 1:
                            act.wait_ge(s["inproj_mm"], DC * b)
                        copy(ctxT[:, m, :], ps[:, 4 + m, :], s["ctxT_ready"])
                elif kind == "xpad":
                    if b == 0 and c == 0:
                        act.wait_ge(s["const_set"], 4)
                    act.wait_ge(s["inproj_mm"], DC * b + c + 1)
                    if b >= 1:
                        act.wait_ge(s["conv_done"], DC * (b - 1) + c + 1)
                        act.wait_ge(s["xdbl_mm"], b)
                        act.wait_ge(s["dtu_ready"], b)
                    nc.scalar.activation(u[:, c, :], ps[:, 4 + c % 2, :], ACT.Identity, bias=vec[:, c:c + 1],
                                         scale=cw[:, c, TAPS - 1:TAPS])
                    copy(xpad[:, c, TAPS - 1:XP], ps[:, 4 + c % 2, :], s["xpad_ready"])
                elif kind == "tanh":
                    if b >= 1:
                        act.wait_ge(s["dt_ready"], b)
                    act.wait_ge(s["conv_done"], DC * b + c + 1)
                    nc.scalar.activation(bt1[:, c, :], u[:, c, :], ACT.Tanh).then_inc(s["tanh_ready"], 1)
                elif kind == "xdbl":
                    act.wait_ge(s["xdbl_mm"], b + 1)
                    if b >= 1:
                        act.wait_ge(s["dt_mm"], DC * b)
                        act.wait_ge(s["bc_st"], 16 * b)
                    copy(xdbl[:], ps[0:DR + 2 * NS, 4, :], s["xdbl_ready"])
                elif kind == "xs":
                    act.wait_ge(s["dt_mm"], DC * b + c + 1)
                    nc.scalar.activation(dt[p][:, c, :], ps[:, 5 - c % 2, :], ACT.Identity,
                                         bias=vec[:, DC + c:DC + c + 1]).then_inc(s["xs_done"], 1)
                elif kind == "exp":
                    act.wait_ge(s["xm_ready"], b + 1)
                    act.wait_ge(s["u_ready"], DC * (b + 1))
                    nc.scalar.activation(bt1[:], dtu[p], ACT.Exp).then_inc(s["e_ready"], 1)
                elif kind == "ln":
                    act.wait_ge(s["ser_ready"], DC * (b + 1))
                    nc.scalar.activation(bt1[:], bt1[:], ACT.Ln, bias=1.0).then_inc(s["l_ready"], 1)
                elif kind == "du":
                    act.wait_ge(s["dt_ready"], b + 1)
                    act.wait_ge(s["u_ready"], DC * (b + 1))
                    nc.scalar.activation(bt2[:, c, :], u[:, c, :], ACT.Copy,
                                         scale=vec[:, 2 * DC + c:2 * DC + c + 1]).then_inc(s["du_ready"], 1)
                elif kind == "dA":
                    q = b * STEPS + c
                    g, k = divmod(c, DC)
                    act.wait_ge(s["dt_ready"], b + 1)
                    if q >= 2:
                        act.wait_ge(s["scan_done"], q - 1)
                    for n in range(NB):
                        a = nc.scalar.activation(dA[q % 2][:, n, 1:L], dt[p][:, k, 1:L], ACT.Exp,
                                                 scale=An[:, k, NB * g + n:NB * g + n + 1])
                    a.then_inc(s["dA_done"], 1)
                elif kind == "gate":
                    act.wait_ge(s["gsc_ready"], 2 * b + 1)
                    if c % 2 in used:
                        act.wait_ge(*used[c % 2])
                    if b >= 1:
                        act.wait_ge(s["xnT_mm"], HC * b)
                        act.wait_ge(s["xn_st"], 16 * b)
                    for dst, f in ((zx[:, c, :], ACT.Identity), (tg[c % 2][:], ACT.Tanh)):
                        a = nc.scalar.activation(dst, xb[p][:, c, :], f, bias=gsc[:, c, 1:2], scale=gsc[:, c, 0:1])
                    a.then_inc(s["gth_ready"], 1)
                    used[c % 2] = (s["zg_ready"], LT * b + c + 1)
                elif kind == "zT":
                    act.wait_ge(s["zT_mm"], LT * b + c + 1)
                    if b >= 1:
                        act.wait_ge(s["yz_done"], LT * b)
                    copy(zT[:, c, :], ps[:, 4 + c % 2, :], s["zT_ready"])
                elif kind == "xn":
                    act.wait_ge(s["gsc_ready"], 2 * b + 2)
                    act.wait_ge(s["zT_mm"], LT * (b + 1))
                    nc.scalar.activation(zx[:, c, :], xb[p][:, c, :], ACT.Identity, bias=gsc[:, c, 1:2],
                                         scale=gsc[:, c, 0:1]).then_inc(s["xn_ready"], 1)
                elif kind == "xnT":
                    act.wait_ge(s["xnT_mm"], HC * b + c + 1)
                    if b >= 1:
                        act.wait_ge(s["gu_mm"], NI * b)
                        act.wait_ge(s["lg_mm"], LT * b)
                    copy(xnT[:, c, :], ps[:, 4 + c % 2, :], s["xnT_ready"])
                elif kind == "logits":
                    n = LT * b + c
                    act.wait_ge(s["lg_mm"], n + 1)
                    if n >= 1:
                        act.wait_ge(s["slot_ready"], n)
                    copy(lg[:], ps[:, 4, 0:E], s["lg_ready"])
                elif kind == "weights":
                    n = LT * b + c
                    act.wait_ge(s["m_ready"], n + 1)
                    act.wait_ge(s["lg_ready"], n + 1)
                    nc.scalar.activation(ohp[:, 0, :], lg[:], ACT.Exp, bias=negm[:], accum_out=ssum[:])
                    nc.scalar.activation(e6[:], m8[:, 0:K], ACT.Exp, bias=negm[:]).then_inc(s["ex_ready"], 1)
                elif kind == "shared":
                    m = ISC[c]
                    act.wait_ge(s["g_mm"], NI * b + c + 1)
                    if c % 2 in used:
                        act.wait_ge(*used[c % 2])
                    nc.scalar.activation(tg[c % 2][0:m, :], ps[0:m, 6, :], ACT.Tanh, scale=0.5)\
                        .then_inc(s["sth_ready"], 1)
                    used[c % 2] = (s["hs_ready"], NI * b + c + 1)

            def evac_tokens(i, j, first=False):
                act.wait_ge(s["xgT_mm"], 2 * i + j + 1)
                if not first:
                    act.wait_ge(s["egu_mm"], 2 * i + j - 1)
                copy(xgT[j], ps[:, 0, :].rearrange("p (c t) -> p c t", c=HC), s["xgT_ready"])

            def silu(i, j, first=False):
                act.wait_ge(s["egu_mm"], 2 * i + j + 1)
                if not first:
                    act.wait_ge(s["hT_mm"], 2 * i + j - 1)
                nc.scalar.activation(hh[j][:, 0:I], ps[:, 2 + j, 0:I], ACT.Silu).then_inc(s["silu_ready"], 1)

            def evac_acts(i, j, first=False):
                act.wait_ge(s["hT_mm"], 2 * i + j + 1)
                if not first:
                    act.wait_ge(s["y_mm"], 2 * i + j - 1)
                copy(hT[j], ps[:, 1, 0:IC * P].rearrange("p (c t) -> p c t", c=IC), s["hT_ready"])

            evac_tokens(0, 0, True)
            evac_tokens(0, 1, True)
            silu(0, 0, True)
            evac_acts(0, 0, True)
            evac_tokens(1, 0)
            silu(0, 1, True)
            evac_acts(0, 1, True)
            with act.Fori(1, NPAIR // 2 - 1) as i:
                evac_tokens(i, 1)
                silu(i, 0)
                evac_acts(i, 0)
                evac_tokens(i + 1, 0)
                silu(i, 1)
                evac_acts(i, 1)
            i = NPAIR // 2 - 1
            evac_tokens(i, 1)
            silu(i, 0)
            evac_acts(i, 0)
            silu(i, 1)
            evac_acts(i, 1)

        @block.vector
        def _(dve):
            count = [0]

            def link(ins):
                count[0] += 1
                ins.then_inc(s["dve"], 1)
                dve.wait_ge(s["dve"], count[0])

            V = nc.vector

            link(V.memset(zeros, 0.0))
            link(V.memset(csum[:], 0.0))
            for a in dA:
                link(V.memset(a[:, :, 0:1], 0.0))
            link(V.memset(xpad[:, :, 0:TAPS - 1], 0.0))
            dve.wait_ge(s["par_in"], 16 * 9)
            link(V.tensor_scalar(cw[:], cw[:], 0.5, None, ALU.mult))
            dve.wait_ge(s["pre_ev"], 6)
            link(V.tensor_scalar(vec[:, 0:DC], vec[:, 0:DC], 0.5, None, ALU.mult))
            dve.wait_ge(s["a_exp"], 1)
            V.tensor_scalar(An[:], An[:], -1.0, None, ALU.mult).then_inc(s["const_set"], 1)

            def scan(q, b, c):
                dve.wait_ge(s["dA_done"], q + 1)
                dve.wait_ge(s["dbu_done"], q + 1)
                V.tensor_tensor_scan(S[q % 4].rearrange("p n l -> p (n l)"), dA[q % 2].rearrange("p n l -> p (n l)"),
                                     S[q % 4].rearrange("p n l -> p (n l)"), 0.0, ALU.mult, ALU.add)\
                    .then_inc(s["scan_done"], 1)

            def weigh(q):
                n = q // DC
                dve.wait_ge(s["scan_done"], q + 1)
                dve.wait_ge(rep_in[n % 2], 32 * (n // 2 + 1))
                V.tensor_tensor(S[q % 4], S[q % 4], Crep[n % 2], ALU.mult).then_inc(s["cs_done"], 1)

            for kind, b, c in mine("dve"):
                p = b % 2
                if kind == "conv":
                    a = u[:, c, :]
                    dve.wait_ge(s["xpad_ready"], DC * b + c + 1)
                    for k in range(TAPS - 1):
                        ins = V.scalar_tensor_tensor(a, xpad[:, c, k:k + L], cw[:, c, k:k + 1], a,
                                                     ALU.mult, ALU.add)
                        if k < TAPS - 2:
                            link(ins)
                    ins.then_inc(s["conv_done"], 1)
                elif kind == "u":
                    dve.wait_ge(s["tanh_ready"], DC * b + c + 1)
                    V.scalar_tensor_tensor(u[:, c, :], bt1[:, c, :], 1.0, u[:, c, :], ALU.add, ALU.mult)\
                        .then_inc(s["u_ready"], 1)
                elif kind == "xm":
                    dve.wait_ge(s["xs_done"], DC * (b + 1))
                    if b >= 2:
                        dve.wait_ge(s["dbu_done"], STEPS * (b - 1))
                    V.tensor_scalar(dtu[p], dt[p], 40.0, None, ALU.min).then_inc(s["xm_ready"], 1)
                elif kind == "softplus":
                    dve.wait_ge(s["l_ready"], b + 1)
                    link(V.copy_predicated(bt1[:], bt2[:].bitcast(U32), dtu[p]))
                    V.tensor_tensor(dt[p], dt[p], bt1[:], ALU.max).then_inc(s["dt_ready"], 1)
                    dve.wait_ge(s["dt_ready"], b + 1)
                    V.tensor_tensor(dtu[p], dt[p], u, ALU.mult).then_inc(s["dtu_ready"], 1)
                elif kind == "scan":
                    scan(b * STEPS + c, b, c)
                elif kind == "weigh":
                    weigh(b * STEPS + c)
                elif kind in ("gate_stats", "x2"):
                    if kind == "gate_stats":
                        dve.wait_ge(x_in[p], 16 * (b // 2 + 1))
                    else:
                        dve.wait_ge(s["yz_done"], LT * b + c + 1)
                        link(V.tensor_tensor(xb[p][:, c, :], xb[p][:, c, :], zT[:, c, :], ALU.add))
                    link(V.bn_stats(stats[:, c, :], xb[p][:, c, :]))
                    link(V.bn_aggr(mv[:, c, :], stats[:, c, :]))
                elif kind in ("gate_var", "var"):
                    if kind == "var":
                        dve.wait_ge(s["zg_ready"], LT * (b + 1))
                    V.tensor_scalar(gsc[:, :, 0], mv[:, :, 1], EPS, None, ALU.add).then_inc(s["var_ready"], 1)
                elif kind in ("gate_scale", "scale"):
                    dve.wait_ge(s["rstd_ready"], 2 * b + 1 + (kind == "scale"))
                    if kind == "gate_scale":
                        link(V.tensor_scalar(gsc[:, :, 0], gsc[:, :, 0], 0.5, None, ALU.mult))
                    V.scalar_tensor_tensor(gsc[:, :, 1], mv[:, :, 0], -1.0, gsc[:, :, 0], ALU.mult, ALU.mult)\
                        .then_inc(s["gsc_ready"], 1)
                elif kind == "gate":
                    dve.wait_ge(s["gth_ready"], LT * b + c + 1)
                    V.scalar_tensor_tensor(zx[:, c, :], tg[c % 2][:], 1.0, zx[:, c, :], ALU.add, ALU.mult)\
                        .then_inc(s["zg_ready"], 1)
                elif kind == "yz":
                    dve.wait_ge(s["yT_done"], STEPS * (b + 1))
                    dve.wait_ge(s["zT_ready"], LT * (b + 1))
                    for t in range(LT):
                        V.tensor_tensor(zT[:, t, :], ps_y[:, t, :], zT[:, t, :], ALU.mult).then_inc(s["yz_done"], 1)
                elif kind == "choose":
                    n = LT * b + c
                    if n == 0:
                        dve.wait_ge(s["iota_set"], 1)
                    dve.wait_ge(s["lg_ready"], n + 1)
                    link(V.max(m8[:], lg[:]))
                    V.tensor_scalar(negm[:], m8[:, 0:1], -1.0, None, ALU.mult).then_inc(s["m_ready"], 1)
                    link(V.max_index(i8[:], m8[:], lg[:]))
                    link(V.tensor_copy(i8f[:], i8[:, 0:K]))
                    link(V.tensor_tensor(oh[:], iota_e[:, None, :].to_broadcast([P, K, E]),
                                         i8f[:, :, None].to_broadcast([P, K, E]), ALU.is_equal))
                    if n >= 1:
                        dve.wait_ge(s["pos_mm"], n)
                        link(V.tensor_tensor(csum[:], csum[:], mask[:], ALU.add))
                    with nc.allow_low_precision("sums of one-hot rows, exact"):
                        V.tensor_reduce(mask[:], oh[:].rearrange("p k e -> p e k"), AX_X, ALU.add)\
                            .then_inc(s["mask_ready"], 1)
                elif kind == "slots":
                    n = LT * b + c
                    dve.wait_ge(s["ex_ready"], n + 1)
                    link(V.reciprocal(ssum[:], ssum[:]))
                    link(V.tensor_scalar(rec[:, n, :, 1], e6[:], ssum[:], None, ALU.mult))
                    V.tensor_copy(rec[:, n, :, 0], tokid[:, n:n + 1].to_broadcast([P, K]))
                    dve.wait_ge(s["pos_mm"], n + 1)
                    link(V.tensor_tensor(ohp[:], oh[:], ps[:, 5, None, 0:E].to_broadcast([P, K, E]), ALU.mult))
                    link(V.tensor_reduce(posk[:], ohp[:], AX_X, ALU.add))
                    link(V.scalar_tensor_tensor(slotf[:], i8f[:], float(CAP), posk[:], ALU.mult, ALU.add))
                    link(V.tensor_scalar(over[:], posk[:], float(CAP), float(2 * E * CAP), ALU.is_ge, ALU.mult))
                    V.tensor_tensor(slotu[:, n, :], slotf[:], over[:], ALU.add).then_inc(s["slot_ready"], 1)
                elif kind == "shared":
                    m = ISC[c]
                    th = tg[c % 2][0:m, :]
                    dve.wait_ge(s["sth_ready"], NI * b + c + 1)
                    if b >= 1:
                        dve.wait_ge(s["dn_mm"], LT * b)
                    link(V.scalar_tensor_tensor(th, th, 1.0, ps[0:m, 6, :], ALU.add, ALU.mult))
                    dve.wait_ge(s["gu_mm"], NI * b + c + 1)
                    V.scalar_tensor_tensor(hs[0:m, c, :], th, 0.5, ps[0:m, 7, :], ALU.mult, ALU.mult)\
                        .then_inc(s["hs_ready"], 1)
                elif kind == "down":
                    dve.wait_ge(s["dn_mm"], LT * b + c + 1)
                    V.tensor_tensor(xb[p][:, c, :], xb[p][:, c, :], ps[:, 6 + c % 2, :], ALU.add)\
                        .then_inc(s["ob_ready"], 1)
                elif kind == "pads":
                    dve.wait_ge(s["yT_done"], B * STEPS)
                    for j in range(2):
                        V.memset(wd[j][96:P, :, 2, :], 0.0).then_inc(s["pad_set"], 1)
                        V.memset(hh[j][:, I:IC * P], 0.0)

            dve.wait_ge(s["tab_mm"], 1)
            V.tensor_copy(ids[:, :, 0], ps[:, 4, 0:NPAIR]).then_inc(s["ids_ready"], 1)
            V.tensor_copy(wts[:], ps[:, 4, 64:64 + NPAIR]).then_inc(s["ids_ready"], 1)
            V.tensor_copy(ids[0:CAP, :, 1], ps[0:CAP, 4, 128:128 + NPAIR]).then_inc(s["ids_ready"], 1)
            V.tensor_copy(ids[0:CAP, :, 2], ps[0:CAP, 4, 192:192 + NPAIR]).then_inc(s["ids_ready"], 1)
            dve.wait_ge(s["ids_ready"], 4)

            def at_pair(t, i, j):
                if isinstance(i, int):
                    return t[:, 2 * i + j:2 * i + j + 1]
                return t[:, bass.ds(2 * i + j, 1)]

            def index(i, j, first=False):
                if not first:
                    dve.wait_ge(s["xgT_mm"], 2 * i + j - 1)
                V.tensor_copy(idxg[j][:], at_pair(ids[:, :, 0], i, j)).then_inc(s["idx_ready"], 1)

            def gated(i, j):
                dve.wait_ge(s["silu_ready"], 2 * i + j + 1)
                V.tensor_tensor(hh[j][:, 0:I], hh[j][:, 0:I], ps[:, 4 + j, 0:I], ALU.mult).then_inc(s["h_ready"], 1)

            def weighted(i, j, first=False):
                dve.wait_ge(s["y_mm"], 2 * i + j + 1)
                if not first:
                    dve.wait_ge(s["sc_odd"], 16 * (2 * i + j - 1))
                for e in range(2):
                    V.tensor_copy(idxs[j][:, e:e + 1], at_pair(ids[0:CAP, :, 1 + e], i, j))
                V.tensor_copy(wcol[j][:], at_pair(wts, i, j)).then_inc(s["w_ready"], 1)
                dve.wait_ge(s["w_ready"], 2 * i + j + 1)
                V.tensor_scalar(ys[j], ps[:, 6 + j, :], wcol[j][:], None, ALU.mult).then_inc(s["y_ready"], 1)

            index(0, 0, True)
            index(0, 1, True)
            index(1, 0)
            gated(0, 0)
            index(1, 1)
            gated(0, 1)
            weighted(0, 0, True)

            def two_pairs(i, first=False):
                index(i + 1, 0)
                gated(i, 0)
                weighted(i - 1, 1, first)
                index(i + 1, 1)
                gated(i, 1)
                weighted(i, 0)

            two_pairs(1, True)
            with dve.Fori(2, NPAIR // 2 - 1) as i:
                two_pairs(i)
            i = NPAIR // 2 - 1
            gated(i, 0)
            weighted(i - 1, 1)
            gated(i, 1)
            weighted(i, 0)
            weighted(i, 1)

        @block.gpsimd
        def _(pool):
            G = nc.gpsimd
            G.iota(initrow[:, :, 0], pattern=[[1, CAP]], base=TRASH, channel_multiplier=0,
                   allow_small_or_imprecise_dtypes=True)
            G.memset(initrow[:, :, 1], 0.0)
            pool.wait_ge(s["dve"], 1)
            G.memset(ones[:], 1.0).then_inc(s["const_set"], 1)
            G.memset(ident[:], 0.0)
            G.memset(ltri[:], 1.0).then_inc(s["ser_chain"], 1)
            pool.wait_ge(s["ser_chain"], 1)
            G.affine_select(out=ident[:], in_=ident[:], compare_op=ALU.not_equal, fill=1.0, base=0,
                            pattern=[[-1, P]], channel_multiplier=1).then_inc(s["const_set"], 1)
            G.affine_select(out=ltri[:], in_=ltri[:], compare_op=ALU.is_gt, fill=0.0, base=0,
                            pattern=[[1, P]], channel_multiplier=-1).then_inc(s["const_set"], 1)
            G.memset(mhalf[:], -0.5)
            G.iota(iota_e[:], pattern=[[1, E]], base=0, channel_multiplier=0, allow_small_or_imprecise_dtypes=True)
            G.iota(tokid[:], pattern=[[P, B * LT]], base=0, channel_multiplier=1,
                   allow_small_or_imprecise_dtypes=True).then_inc(s["iota_set"], 1)
            chain = [1]

            def link(ins):
                chain[0] += 1
                ins.then_inc(s["ser_chain"], 1)
                pool.wait_ge(s["ser_chain"], chain[0])

            for kind, b, c in mine("pool"):
                p = b % 2
                if kind in ("gate_rstd", "rstd"):
                    pool.wait_ge(s["var_ready"], 2 * b + 1 + (kind == "rstd"))
                    G.tensor_tensor(gsc[:, :, 0], gsc[:, :, 0], mhalf[:], ALU.pow).then_inc(s["rstd_ready"], 1)
                elif kind == "series":
                    pool.wait_ge(s["e_ready"], b + 1)
                    if b == 0:
                        pool.wait_ge(s["init_in"], 16 * 3)
                    else:
                        pool.wait_ge(s["duT_done"], b)
                    e, low, sr = bt1[:, c, :], bt2[:, c, :], dtu[p][:, c, :]
                    link(G.tensor_scalar(low, e, SERIES_BELOW, None, ALU.min))
                    link(G.tensor_scalar(sr, low, -0.25, 1.0 / 3.0, ALU.mult, ALU.add))
                    link(G.tensor_tensor(sr, sr, low, ALU.mult))
                    link(G.tensor_scalar(sr, sr, -0.5, None, ALU.add))
                    link(G.tensor_tensor(sr, sr, low, ALU.mult))
                    link(G.tensor_scalar(sr, sr, 1.0, None, ALU.add))
                    link(G.tensor_tensor(sr, sr, low, ALU.mult))
                    G.tensor_scalar(low, e, SERIES_BELOW, None, ALU.is_lt).then_inc(s["ser_ready"], 1)
                elif kind == "dbu":
                    q = b * STEPS + c
                    n, k = divmod(q, DC)
                    pool.wait_ge(s["dtu_ready"], b + 1)
                    pool.wait_ge(rep_in[n % 2], 32 * (n // 2 + 1))
                    if q >= 4:
                        pool.wait_ge(s["yT_done"], q - 3)
                    G.tensor_tensor(S[q % 4], dtu[p][:, k, None, :].to_broadcast([P, NB, L]), Brep[n % 2], ALU.mult)\
                        .then_inc(s["dbu_done"], 1)
                elif kind == "scatter":
                    n = LT * b + c
                    pool.wait_ge(s["slot_ready"], n + 1)
                    for k in range(K):
                        G.indirect_dma_start(
                            out=slot_dram, out_offset=bass.IndirectOffsetOnAxis(ap=slotu[:, n, k:k + 1], axis=0),
                            in_=rec[:, n, k, :], in_offset=None, bounds_check=E * CAP - 1, oob_is_err=False)\
                            .then_inc(s["scattered"], 16)

            pool.wait_ge(s["xn_st"], 16 * B)
            pool.wait_ge(s["out_st"], 16 * B)

            def hold():
                pool.sem_inc(s["held"], 1)

            def gather(i, j, first=False):
                pool.wait_ge(s["idx_ready"], 2 * i + j + 1)
                if not first:
                    pool.wait_ge(s["xgT_mm"], 2 * i + j - 1)
                hold()
                G.indirect_dma_start(out=xg[j], out_offset=None, in_=xn_dram,
                                     in_offset=bass.IndirectOffsetOnAxis(ap=idxg[j][:], axis=0),
                                     bounds_check=T + CAP - 1, oob_is_err=True).then_inc(xg_in[j], 16)

            def scatter(i, j, first=False):
                pool.wait_ge(s["y_ready"], 2 * i + j + 1)
                if not first:
                    pool.wait_ge(s["sc_odd"], 16 * (2 * i + j))
                for e, done in ((0, s["sc_even"]), (1, s["sc_odd"])):
                    if e == 1:
                        pool.wait_ge(s["sc_even"], 16 * (2 * i + j + 1))
                    hold()
                    G.indirect_dma_start(out=out, out_offset=bass.IndirectOffsetOnAxis(
                        ap=idxs[j][:, e:e + 1], axis=0), in_=ys[j][64 * e:64 * e + 64, :], in_offset=None,
                        bounds_check=T + CAP - 1, oob_is_err=True, compute_op=ALU.add).then_inc(done, 16)

            gather(0, 0, True)
            gather(0, 1, True)
            gather(1, 0)
            scatter(0, 0, True)
            gather(1, 1)
            scatter(0, 1)
            with pool.Fori(1, NPAIR // 2 - 1) as i:
                gather(i + 1, 0)
                scatter(i, 0)
                gather(i + 1, 1)
                scatter(i, 1)
            for j in range(2):
                scatter(NPAIR // 2 - 1, j)


_INS = ['x', 'ctx_1024', 'L0_xattn_in_proj_w', 'L0_xattn_conv_w', 'L0_xattn_conv_b', 'L0_xattn_x_proj_w',
        'L0_xattn_dt_proj_w', 'L0_xattn_dt_proj_b', 'L0_xattn_A_log', 'L0_xattn_D', 'L0_ffn_gate_w',
        'L0_ffn_w_gate', 'L0_ffn_w_up', 'L0_ffn_w_down', 'L0_ffn_sw_gate', 'L0_ffn_sw_up', 'L0_ffn_sw_down']


def kernel(**inputs):
    import numpy as np
    import concourse.bacc as bacc
    from concourse.bass_utils import run_bass_kernel_spmd

    nc = bacc.Bacc("TRN2", target_bir_lowering=False, num_devices=1, dynamic_dma_scratch_size=4096)
    arrays, args = {}, []
    for name in _INS:
        a = np.ascontiguousarray(inputs[name])
        arrays[f"in_{name}"] = a
        args.append(nc.dram_tensor(f"in_{name}", a.shape, mybir.dt.from_np(a.dtype), kind="ExternalInput").ap())
    out = nc.dram_tensor("out_rows", [T + CAP, H], F32, kind="ExternalOutput").ap()
    build(nc, *args, out)
    r = run_bass_kernel_spmd(nc, [arrays], core_ids=[0])
    return r.results[0]["out_rows"][:T].reshape(B, L, H)
```

```python
from contextlib import ExitStack

import concourse.bass as bass
from concourse import mybir

F32 = mybir.dt.float32
BF16 = mybir.dt.bfloat16
U32 = mybir.dt.uint32
ALU = mybir.AluOpType
ACT = mybir.ActivationFunctionType
AX_X = mybir.AxisListType.X

P = 128
B, L, H = 4, 512, 512
DM, DI, NS, DR = 256, 512, 16, 16
TAPS = 4
E, K, I, CAP = 64, 6, 352, 64
IS = 704
T = B * L
EPS = 1e-5
DC = DI // P
LT = L // P
HC = H // P
NB = 2
NG = NS // NB
STEPS = NG * DC
ISC = [P] * (IS // P) + [IS % P]
NI = len(ISC)
NPAIR = E // 2
IC = 3
IREST = I - 2 * P
PIECES = 8
FLY = 3
TRASH = T
SERIES_BELOW = 0.03


def build(nc, x, ctx_1024, in_proj_w, conv_w, conv_b, x_proj_w, dt_proj_w, dt_proj_b, A_log, D,
          gate_w, w_gate, w_up, w_down, sw_gate, sw_up, sw_down, out):
    bc_dram = nc.dram_tensor("bc_rows", [B, 2 * NS, L], F32, kind="Internal").ap()
    xn_dram = nc.dram_tensor("xn_rows", [T + P, H], F32, kind="Internal").ap()
    slot_dram = nc.dram_tensor("slot_table", [E * CAP, 2], F32, kind="Internal").ap()

    with ExitStack() as ctx:
        ctx.enter_context(nc.allow_non_contiguous_dma(reason="small parameter loads"))

        def sb(name, shape, dt=F32):
            return ctx.enter_context(nc.sbuf_tensor(name, shape, dt))

        def sem(name):
            return ctx.enter_context(nc.semaphore(name))

        GW = 2 * HC * I
        DWN = 2 * IC * H
        PAIRW = 2 * GW + DWN
        arena = sb("arena", [P, 2 * PAIRW])
        at = [0]

        def carve(t, words):
            a = t[:, at[0]:at[0] + words]
            at[0] += words
            return a

        dA = [carve(arena, NB * L).rearrange("p (n l) -> p n l", n=NB) for _ in range(2)]
        S = [carve(arena, NB * L).rearrange("p (n l) -> p n l", n=NB) for _ in range(3)]
        S.append(sb("S3", [P, NB, L])[:])
        Brep = [carve(arena, NB * L).rearrange("p (n l) -> p n l", n=NB) for _ in range(2)]
        Crep = [carve(arena, NB * L).rearrange("p (n l) -> p n l", n=NB) for _ in range(2)]
        dt = [carve(arena, DC * L).rearrange("p (c l) -> p c l", c=DC) for _ in range(2)]
        dtu = [carve(arena, DC * L).rearrange("p (c l) -> p c l", c=DC) for _ in range(2)]
        assert at[0] <= 2 * PAIRW
        at[0] = 0
        wg, wu, wd = [], [], []
        for j in range(2):
            wg.append(carve(arena, GW).rearrange("p (e c i) -> p e c i", e=2, c=HC))
            wu.append(carve(arena, GW).rearrange("p (e c i) -> p e c i", e=2, c=HC))
            wd.append(carve(arena, DWN).rearrange("p (e c h) -> p e c h", e=2, c=IC))

        XP = L + TAPS - 1
        prep = sb("prep", [P, DC * L + DC * XP + LT * DM + 2 * L])
        at[0] = 0
        u = carve(prep, DC * L).rearrange("p (c l) -> p c l", c=DC)
        xpad = carve(prep, DC * XP).rearrange("p (c l) -> p c l", c=DC)
        cin = carve(prep, LT * DM).rearrange("p (t d) -> p t d", t=LT)
        ctxT = carve(prep, 2 * L).rearrange("p (m l) -> p m l", m=2)
        at[0] = 0
        xg, xgT, hh, hT = [], [], [], []
        for j in range(2):
            xg.append(carve(prep, H))
            xgT.append(carve(prep, H).rearrange("p (c t) -> p c t", c=HC))
            hh.append(carve(prep, IC * P))
            hT.append(carve(prep, (IC + 1) * P).rearrange("p (c t) -> p c t", c=IC + 1))
        tab = carve(prep, 2 * P)[0:NPAIR]
        ids = carve(prep, NPAIR).bitcast(U32)
        meta = carve(prep, 3 * NPAIR).rearrange("p (q k) -> p q k", k=3)

        xb = [sb(f"xb{j}", [P, LT, H]) for j in range(2)]
        zx = sb("zx", [P, LT, H])
        zT = sb("zT", [P, LT, DI])
        xnT = sb("xnT", [P, HC, L])
        hs = sb("hs", [P, NI, L])
        swg = sb("swg", [P, HC, IS])
        swu = sb("swu", [P, HC, IS])
        swd = sb("swd", [P, NI, H])
        bt1 = sb("bt1", [P, DC, L])
        bt2 = sb("bt2", [P, DC, L])
        yw = [bt1[:, j, :] for j in range(2)]
        ys = [bt1[:, 2 + j, :] for j in range(2)]
        tg = [sb(f"tg{j}", [P, L]) for j in range(2)]
        winT = sb("winT", [P, 2, DI])
        xpT = sb("xpT", [P, DC, DR + 2 * NS])
        dtwT = sb("dtwT", [DR, DI])
        xdbl = sb("xdbl", [DR + 2 * NS, L])
        gwT = sb("gwT", [P, HC, E])
        ident = sb("ident", [P, P])
        ltri = sb("ltri", [P, P], BF16)
        ones = sb("ones", [P, P], BF16)
        vec = sb("vec", [P, 3 * DC])
        cw = sb("cw", [P, DC, TAPS])
        An = sb("An", [P, DC, NS])
        stats = sb("stats", [P, LT, 6])
        mv = sb("mv", [P, LT, 2])
        gsc = sb("gsc", [P, LT, 2])
        mhalf = sb("mhalf", [P, LT])
        iota_e = sb("iota_e", [P, E])
        tokid = sb("tokid", [P, B * LT])
        csum = sb("csum", [P, E], BF16)
        mask = sb("mask", [P, E], BF16)
        lg = sb("lg", [P, E])
        m8 = sb("m8", [P, 8])
        i8 = sb("i8", [P, 8], U32)
        i8f = sb("i8f", [P, K])
        negm = sb("negm", [P, 1])
        ssum = sb("ssum", [P, 1])
        e6 = sb("e6", [P, K])
        oh = sb("oh", [P, K, E])
        ohp = sb("ohp", [P, K, E])
        posk = sb("posk", [P, K])
        slotf = sb("slotf", [P, K])
        over = sb("over", [P, K])
        slotu = sb("slotu", [P, B * LT, K], U32)
        rec = sb("rec", [P, B * LT, K, 2])
        idxg = [sb(f"idxg{j}", [P, 1], U32) for j in range(2)]
        idxs = [sb(f"idxs{j}", [P, 1], U32) for j in range(2)]
        mcol = [sb(f"mcol{j}", [P, 3]) for j in range(2)]
        dup = sb("dup", [P, 1])
        sel = [sb(f"sel{j}", [NPAIR, 1]) for j in range(2)]
        spare = sb("spare", [P, 1])
        is_odd = sb("is_odd", [P, 1])
        same = [oh[:].rearrange("p k e -> p (k e)")[:, j * P:(j + 1) * P] for j in range(2)]
        ps = ctx.enter_context(nc.psum_tensor("ps", [P, 8, 512], F32))
        ps_y = ps[:, 0:4, :]

        raw_win = zx[:, 0:2, :].rearrange("p t (c d) -> p (t c) d", d=DM)
        raw_gw = zT[0:E, 0, :]
        raw_xp = zT[0:DR + 2 * NS, 1, :]
        raw_dtw = zT[:, 2, 0:DC * DR].rearrange("p (c r) -> p c r", c=DC)
        raw_vec = zT[0:3 * DC, 3, 0:P]
        zeros = bt2[0:CAP, 0, :]
        initrow = bt2[0:NPAIR, 1, 0:2 * P].rearrange("q (c t) -> q c t", t=2)

        names = """par_in sw_in const_set a_exp iota_set init_in pre_t pre_ev
            ctx_in0 ctx_in1 x_in0 x_in1 bc_st rep_in0 rep_in1 xn_st out_st scattered
            ctxT_mm ctxT_ready inproj_mm xpad_ready conv_done tanh_ready u_ready xdbl_mm xdbl_ready
            dt_mm xs_done xm_ready e_ready ser_chain ser_ready l_ready dt_ready dtu_ready du_ready duT_done
            dA_done dbu_done scan_done cs_done yT_done
            var_ready rstd_ready gsc_ready gth_ready zg_ready zT_mm zT_ready yz_done xn_ready xnT_mm xnT_ready
            lg_mm lg_ready m_ready ex_ready mask_ready pos_mm slot_ready
            g_mm gu_mm sth_ready sa_ready hs_ready dn_mm ob_ready dve
            held sp_held tab_in tab_mm ids_ready idx_ready w_ready sel_ready dup_ready idxs_ready xg_in0 xg_in1 xgT_mm xgT_ready
            egu_mm silu_ready h_ready hT_mm hT_ready y_mm y_ready
             same_ready yw_ready merged_mm scat pad_set""".split()
        s = {n: sem(n) for n in names}
        rep_in = [s["rep_in0"], s["rep_in1"]]
        x_in = [s["x_in0"], s["x_in1"]]
        xg_in = [s["xg_in0"], s["xg_in1"]]
        w_in = [[sem(f"w{j}_in{n}") for n in range(PIECES)] for j in range(2)]

        def first_phase():
            parts = []

            def add(time, engine, kind, b, c=None):
                parts.append((time, len(parts), engine, kind, b, c))

            for q in range(B * STEPS):
                b, step = divmod(q, STEPS)
                add(q - 1.4, "pool", "dbu", b, step)
                add(q - 1.0, "act", "dA", b, step)
                add(q, "dve", "scan", b, step)
                add(q + 1.05, "dve", "weigh", b, step)
                add(q + 1.5, "pe", "yT", b, step)
                if step % DC == DC - 1 and gi(b, step // DC) + 2 < B * NG:
                    add(q + 1.6, "sp", "rep", b, step)
            for b in range(B):
                t = STEPS * (b - 1) + 10 if b else -20
                if b:
                    add(t - 4, "sp", "ctx_load", b)
                add(t, "pe", "ctx", b)
                add(t + 0.4, "act", "ctx", b)
                for c in range(DC):
                    mm = t + 1.6 + 2 * (c // 2)
                    add(mm, "pe", "inproj", b, c)
                    add(mm + 0.4, "act", "xpad", b, c)
                    add(t + 2.5 + c, "dve", "conv", b, c)
                    add(t + 2.8 + c, "act", "tanh", b, c)
                    add(t + 3.2 + c, "dve", "u", b, c)
                    add(t + 7.8 + 0.8 * (c // 2), "pe", "dt", b, c)
                    add(t + 8.2 + 0.8 * (c // 2), "act", "xs", b, c)
                    add(t + 9.6 + 1.7 * c, "pool", "series", b, c)
                add(t + 7, "pe", "xdbl", b)
                add(t + 7.3, "act", "xdbl", b)
                add(t + 7.4, "sp", "xdbl", b)
                add(t + 9.2, "dve", "xm", b)
                add(t + 9.3, "act", "exp", b)
                add(t + 16.5, "act", "ln", b)
                add(t + 16.8, "dve", "softplus", b)
                for c in range(DC):
                    add(t + 18.2 + 0.2 * c, "act", "du", b, c)
                t = STEPS * b
                for c in range(LT):
                    add(t + 8 + c, "dve", "gate_stats", b, c)
                    add(t + 13 + c, "act", "gate", b, c)
                    add(t + 13.5 + c, "dve", "gate", b, c)
                    add(t + 20.4 + 0.5 * (c // 2), "pe", "gate", b, c)
                    add(t + 20.8 + 0.5 * (c // 2), "act", "zT", b, c)
                add(t + 12.2, "dve", "gate_var", b)
                add(t + 12.3, "pool", "gate_rstd", b)
                add(t + 12.6, "dve", "gate_scale", b)
                add(t + 0.7, "pe", "duT", b)
                t = STEPS * (b + 1)
                add(t + 0.6, "dve", "yz", b)
                for c in range(LT):
                    add(t + 1.2 + 0.4 * c, "dve", "x2", b, c)
                    add(t + 3.3 + 0.3 * c, "act", "xn", b, c)
                add(t + 2.7, "dve", "var", b)
                add(t + 2.8, "pool", "rstd", b)
                add(t + 3.1, "dve", "scale", b)
                add(t + 4.6, "sp", "xn", b)
                for c in range(HC):
                    add(t + 5 + c // 2, "pe", "xnT", b, c)
                    add(t + 5.4 + c // 2, "act", "xnT", b, c)
                for c in range(LT):
                    n = t + 7 + 2 * c
                    add(n, "pe", "logits", b, c)
                    add(n + 0.3, "act", "logits", b, c)
                    add(n + 0.6, "dve", "choose", b, c)
                    add(n + 0.9, "act", "weights", b, c)
                    add(n + 1.6, "pe", "pos", b, c)
                    add(n + 2.0, "dve", "slots", b, c)
                    add(n + 2.7, "pool", "scatter", b, c)
                unit = 0
                for c in range(NI):
                    for k in range(4):
                        add(t + 7.1 + 0.66 * unit, "pe", "shared", b, (c, k))
                        unit += 1
                    add(t + 7.1 + 0.66 * unit - 1.2, "act", "shared", b, c)
                    add(t + 7.1 + 0.66 * unit - 0.4, "dve", "shared", b, c)
                for c in range(LT):
                    for k in range(NI // 2):
                        add(t + 7.1 + 0.66 * unit, "pe", "down", b, (c, k))
                        unit += 1
                    add(t + 7.1 + 0.66 * unit - 0.3, "dve", "down", b, c)
                add(t + 31.5, "sp", "out", b)
            add(STEPS * B + 2, "dve", "pads", B - 1)
            add(STEPS * B + 2.1, "sp", "weights", B - 1)
            parts.sort()
            return parts

        def gi(b, g):
            return b * NG + g

        PARTS = first_phase()

        def mine(engine):
            return [(kind, b, c) for _, _, e, kind, b, c in PARTS if e == engine]

        def pick(a, q):
            return a[bass.ds(q, 1)].rearrange("o p f -> (o p) f") if not isinstance(q, int) else a[q]

        def gate_up(sp, q, j, wait=None):
            for n, (w, dst, e) in enumerate(((w_gate, wg, 0), (w_gate, wg, 1), (w_up, wu, 0), (w_up, wu, 1))):
                if wait:
                    wait(n)
                src = w.rearrange("(q e) (p c) i -> q e p (c i)", e=2, c=HC)[:, e]
                sp.dma_start(dst[j][:, e].rearrange("p c i -> p (c i)"), pick(src, q)).then_inc(w_in[j][n], 16)

        def down(sp, q, j, wait=None):
            for e in range(2):
                n = 4 + 2 * e
                if wait:
                    wait(n)
                head = w_down[:, 0:2 * P, :].rearrange("(q e) (p c) h -> q e p (c h)", e=2, c=2)[:, e]
                sp.dma_start(wd[j][:, e, 0:2, :].rearrange("p c h -> p (c h)"), pick(head, q)).then_inc(w_in[j][n], 16)
                if wait:
                    wait(n + 1)
                rest = w_down[:, 2 * P:I, :].rearrange("(q e) p h -> q e p h", e=2)[:, e]
                sp.dma_start(wd[j][0:IREST, e, 2, :], pick(rest, q)).then_inc(w_in[j][n + 1], 16)

        def weights(sp, q, j):
            gate_up(sp, q, j)
            sp.wait_ge(s["pad_set"], 2)
            down(sp, q, j)

        block = ctx.enter_context(nc.Block())

        @block.sync
        def _(sp):
            def load(dst, src, sm):
                return sp.dma_start(dst, src).then_inc(sm, 16)

            load(cin, ctx_1024[0].rearrange("(t p) d -> p t d", p=P), s["ctx_in0"])
            load(raw_win, in_proj_w.rearrange("(c p) d -> p c d", p=P), s["par_in"])
            load(raw_xp, x_proj_w, s["par_in"])
            load(raw_dtw, dt_proj_w.rearrange("(c p) r -> p c r", p=P), s["par_in"])
            load(raw_vec[0:DC], conv_b.rearrange("(c p) -> c p", p=P), s["par_in"])
            load(raw_vec[DC:2 * DC], dt_proj_b.rearrange("(c p) -> c p", p=P), s["par_in"])
            load(raw_vec[2 * DC:3 * DC], D.rearrange("(c p) -> c p", p=P), s["par_in"])
            load(cw[:], conv_w.rearrange("(c p) o k -> p c (o k)", p=P), s["par_in"])
            load(An[:], A_log.rearrange("(c p) n -> p c n", p=P), s["par_in"])
            load(raw_gw, gate_w, s["par_in"])
            load(xb[0][:], x[0].rearrange("(t p) c -> p t c", p=P), x_in[0])
            sp.wait_ge(s["const_set"], 1)
            for a in (xn_dram, out):
                load(a[T:T + P, :].rearrange("(t p) c -> p t c", p=CAP),
                     zeros[:, None, :].to_broadcast([CAP, P // CAP, H]), s["init_in"])
            load(slot_dram.rearrange("(q c) t -> q (c t)", q=NPAIR),
                 initrow.rearrange("q c t -> q (c t)"), s["init_in"])
            load(swg[:], sw_gate.rearrange("(p c) i -> p c i", c=HC), s["sw_in"])
            load(swu[:], sw_up.rearrange("(p c) i -> p c i", c=HC), s["sw_in"])
            load(swd[:, 0:NI - 1, :], sw_down[0:(NI - 1) * P].rearrange("(c p) h -> p c h", p=P), s["sw_in"])
            load(swd[0:IS % P, NI - 1, :], sw_down[(NI - 1) * P:IS], s["sw_in"])

            def rep(b, g):
                n = gi(b, g)
                if g == 0:
                    sp.wait_ge(s["bc_st"], 16 * (b + 1))
                if n >= 2:
                    sp.wait_ge(s["dbu_done"], DC * (n - 1))
                    sp.wait_ge(s["cs_done"], DC * (n - 1))
                for dst, row in ((Brep, 0), (Crep, NS)):
                    src = bc_dram[b:b + 1, row + NB * g:row + NB * (g + 1), :].to_broadcast([P, NB, L])
                    load(dst[n % 2], src, rep_in[n % 2])

            load(xb[1][:], x[1].rearrange("(t p) c -> p t c", p=P), x_in[1])
            for kind, b, c in mine("sp"):
                if kind == "ctx_load":
                    sp.wait_ge(s["ctxT_mm"], 2 * b)
                    load(cin, ctx_1024[b].rearrange("(t p) d -> p t d", p=P), s["ctx_in0"])
                elif kind == "xdbl":
                    sp.wait_ge(s["xdbl_ready"], b + 1)
                    load(bc_dram[b], xdbl[DR:DR + 2 * NS, :], s["bc_st"])
                    if b == 0:
                        rep(0, 0)
                        rep(0, 1)
                elif kind == "rep":
                    n = gi(b, c // DC) + 2
                    rep(n // NG, n % NG)
                elif kind == "out":
                    sp.wait_ge(s["ob_ready"], LT * (b + 1))
                    load(out[b * L:(b + 1) * L].rearrange("(t p) c -> p t c", p=P), xb[b % 2][:], s["out_st"])
                    if b + 2 < B:
                        sp.wait_ge(s["out_st"], 16 * (b + 1))
                        load(xb[b % 2][:], x[b + 2].rearrange("(t p) c -> p t c", p=P), x_in[b % 2])
                elif kind == "xn":
                    sp.wait_ge(s["xn_ready"], LT * (b + 1))
                    load(xn_dram[b * L:(b + 1) * L].rearrange("(t p) c -> p t c", p=P), zx[:], s["xn_st"])
                elif kind == "weights":
                    sp.wait_ge(s["yT_done"], B * STEPS)
                    sp.wait_ge(s["dA_done"], B * STEPS)
                    for j in range(2):
                        weights(sp, j, j)
            sp.wait_ge(s["scattered"], 16 * B * LT * K)
            load(tab[:], slot_dram.rearrange("(q c) t -> q (c t)", q=NPAIR), s["tab_in"])

            def free_then_load(i, j):
                def through(n):
                    k = n - FLY
                    if k >= 0:
                        sp.wait_ge(w_in[j][k], 16 * (i + 1))
                    elif j:
                        sp.wait_ge(w_in[0][k + PIECES], 16 * (i + 1))
                    else:
                        sp.wait_ge(w_in[1][k + PIECES], 16 * i)
                    sp.sem_inc(s["sp_held"], 1)

                sp.wait_ge(s["egu_mm"], 2 * i + j - 1)
                sp.sem_inc(s["sp_held"], 1)
                gate_up(sp, 2 * i + j, j, through)
                sp.wait_ge(s["y_mm"], 2 * i + j - 1)
                sp.sem_inc(s["sp_held"], 1)
                down(sp, 2 * i + j, j, through)

            with sp.Fori(1, NPAIR // 2) as i:
                for j in range(2):
                    free_then_load(i, j)
            sp.wait_ge(s["scat"], 16 * NPAIR)
            sp.wait_ge(s["out_st"], 16 * B)
            sp.wait_ge(s["xn_st"], 16 * B)
            sp.wait_ge(s["init_in"], 16 * 3)

        @block.tensor
        def _(pe):
            freed = {}

            def claim(bank):
                if bank in freed:
                    pe.wait_ge(*freed[bank])

            def transpose(dst, src, **kw):
                k = src.shape[0]
                return nc.tensor.matmul(dst, src, ident[0:k, 0:k], is_transpose=True, **kw)

            def flip(bank, cols, srcs, **kw):
                for n, a in enumerate(srcs):
                    m, k = a.shape[1], a.shape[0]
                    last = transpose(ps[0:m, bank, cols + n * k:cols + (n + 1) * k], a, start=True, stop=True)
                return last

            pe.wait_ge(s["const_set"], 3)
            pe.wait_ge(s["par_in"], 16 * 9)
            for m in range(2):
                flip(4 + m, 0, [raw_win[:, c, m * P:(m + 1) * P] for c in range(DC)]).then_inc(s["pre_t"], 1)
            flip(6, 0, [raw_gw[:, c::HC] for c in range(HC)]).then_inc(s["pre_t"], 1)
            flip(7, 0, [raw_xp[:, c * P:(c + 1) * P] for c in range(DC)])
            flip(7, 256, [raw_vec]).then_inc(s["pre_t"], 1)
            pe.wait_ge(s["pre_ev"], 2)
            flip(4, 0, [raw_dtw[:, c, :] for c in range(DC)]).then_inc(s["pre_t"], 1)
            freed.update({4: (s["pre_ev"], 6), 5: (s["pre_ev"], 6), 6: (s["pre_ev"], 6), 7: (s["pre_ev"], 6)})
            pe.wait_ge(s["pre_ev"], 6)

            for kind, b, c in mine("pe"):
                if kind == "ctx":
                    pe.wait_ge(s["ctx_in0"], 16 * (b + 1))
                    for m in range(2):
                        claim(4 + m)
                        flip(4 + m, 0, [cin[:, t, m * P:(m + 1) * P] for t in range(LT)]).then_inc(s["ctxT_mm"], 1)
                        freed[4 + m] = (s["ctxT_ready"], 2 * b + m + 1)
                elif kind == "inproj":
                    bank = 4 + c % 2
                    claim(bank)
                    pe.wait_ge(s["ctxT_ready"], 2 * b + 2)
                    for m in range(2):
                        mm = nc.tensor.matmul(ps[:, bank, :], winT[:, m, c * P:(c + 1) * P], ctxT[:, m, :],
                                              start=(m == 0), stop=(m == 1))
                    mm.then_inc(s["inproj_mm"], 1)
                    freed[bank] = (s["xpad_ready"], DC * b + c + 1)
                elif kind == "xdbl":
                    claim(4)
                    pe.wait_ge(s["u_ready"], DC * (b + 1))
                    for k in range(DC):
                        mm = nc.tensor.matmul(ps[0:DR + 2 * NS, 4, :], xpT[:, k, :], u[:, k, :],
                                              start=(k == 0), stop=(k == DC - 1))
                    mm.then_inc(s["xdbl_mm"], 1)
                    freed[4] = (s["xdbl_ready"], b + 1)
                elif kind == "dt":
                    bank = 5 - c % 2
                    claim(bank)
                    pe.wait_ge(s["xdbl_ready"], b + 1)
                    nc.tensor.matmul(ps[:, bank, :], dtwT[:, c * P:(c + 1) * P], xdbl[0:DR, :],
                                     start=True, stop=True).then_inc(s["dt_mm"], 1)
                    freed[bank] = (s["xs_done"], DC * b + c + 1)
                elif kind == "duT":
                    pe.wait_ge(s["du_ready"], DC * (b + 1))
                    for t in range(LT):
                        if b >= 1:
                            pe.wait_ge(s["yz_done"], LT * (b - 1) + t + 1)
                        for k in range(DC):
                            mm = transpose(ps_y[:, t, k * P:(k + 1) * P], bt2[:, k, t * P:(t + 1) * P],
                                           start=(k == 0), stop=False, skip_group_check=True)
                    mm.then_inc(s["duT_done"], 1)
                elif kind == "yT":
                    q = b * STEPS + c
                    k = c % DC
                    pe.wait_ge(s["cs_done"], q + 1)
                    for n in range(NB):
                        for t in range(LT):
                            mm = transpose(ps_y[:, t, k * P:(k + 1) * P], S[q % 4][:, n, t * P:(t + 1) * P],
                                           start=False, stop=(c >= STEPS - DC and n == NB - 1),
                                           skip_group_check=True)
                    mm.then_inc(s["yT_done"], 1)
                elif kind == "gate":
                    bank = 4 + c % 2
                    claim(bank)
                    pe.wait_ge(s["zg_ready"], LT * (b + 1))
                    flip(bank, 0, [zx[:, k, c * P:(c + 1) * P] for k in range(DC)]).then_inc(s["zT_mm"], 1)
                    freed[bank] = (s["zT_ready"], LT * b + c + 1)
                elif kind == "xnT":
                    pe.wait_ge(s["xn_ready"], LT * (b + 1))
                    bank = 4 + c % 2
                    claim(bank)
                    flip(bank, 0, [zx[:, t, c::HC] for t in range(LT)]).then_inc(s["xnT_mm"], 1)
                    freed[bank] = (s["xnT_ready"], HC * b + c + 1)
                elif kind == "logits":
                    pe.wait_ge(s["xnT_ready"], HC * (b + 1))
                    claim(4)
                    for k in range(HC):
                        mm = nc.tensor.matmul(ps[:, 4, 0:E], xnT[:, k, c * P:(c + 1) * P], gwT[:, k, :],
                                              start=(k == 0), stop=(k == HC - 1))
                    mm.then_inc(s["lg_mm"], 1)
                    freed[4] = (s["lg_ready"], LT * b + c + 1)
                elif kind == "pos":
                    claim(5)
                    pe.wait_ge(s["mask_ready"], LT * b + c + 1)
                    nc.tensor.matmul(ps[:, 5, 0:E], ltri[:], mask[:], start=True, stop=False)
                    nc.tensor.matmul(ps[:, 5, 0:E], ones[:], csum[:], start=False, stop=True).then_inc(s["pos_mm"], 1)
                    freed[5] = (s["slot_ready"], LT * b + c + 1)
                elif kind == "shared":
                    c, half = c
                    m = ISC[c]
                    if b == 0 and c == 0 and half == 0:
                        pe.wait_ge(s["sw_in"], 16 * 4)
                    bank, w = ((6, swg), (7, swu))[half // 2]
                    if half % 2 == 0:
                        pe.wait_ge(s["xnT_ready"], HC * (b + 1))
                        claim(bank)
                    for k in (0, 1) if half % 2 == 0 else (2, 3):
                        mm = nc.tensor.matmul(ps[0:m, bank, :], w[:, k, c * P:c * P + m], xnT[:, k, :],
                                              start=(k == 0), stop=(k == HC - 1))
                    if half % 2:
                        mm.then_inc(s["g_mm" if bank == 6 else "gu_mm"], 1)
                        freed[bank] = (s["hs_ready"], NI * b + c + 1)
                elif kind == "down":
                    c, third = c
                    bank = 6 + c % 2
                    if third == 0:
                        claim(bank)
                        pe.wait_ge(s["hs_ready"], NI * (b + 1))
                    for k in (2 * third, 2 * third + 1):
                        m = ISC[k]
                        mm = nc.tensor.matmul(ps[:, bank, :], hs[0:m, k, c * P:(c + 1) * P], swd[0:m, k, :],
                                              start=(k == 0), stop=(k == NI - 1))
                    if third == NI // 2 - 1:
                        mm.then_inc(s["dn_mm"], 1)
                        freed[bank] = (s["ob_ready"], LT * b + c + 1)

            pe.wait_ge(s["tab_in"], 16)
            claim(4)
            claim(5)
            flip(4, 0, [tab[:, 0::2]])
            flip(4, 64, [tab[:, 1::2]]).then_inc(s["tab_mm"], 1)
            for bank in (6, 7):
                claim(bank)
            pe.wait_ge(s["ids_ready"], 3)
            pe.wait_ge(s["yz_done"], LT * B)

            def tokens(i, j, first=False):
                pe.wait_ge(xg_in[j], 16 * (i + 1))
                if not first:
                    pe.wait_ge(s["xgT_ready"], 2 * i + j)
                flip(0, 0, [xg[j][:, k::HC] for k in range(HC)]).then_inc(s["xgT_mm"], 1)

            def gate_up_mm(i, j, first=False):
                pe.wait_ge(s["xgT_ready"], 2 * i + j + 1)
                for n in range(4):
                    pe.wait_ge(w_in[j][n], 16 * (i + 1))
                if not first:
                    pe.wait_ge(s["h_ready"], 2 * i + j - 1)
                for bank, w in ((2 + j, wg[j]), (4 + j, wu[j])):
                    for k in range(HC):
                        for e in range(2):
                            mm = nc.tensor.matmul(ps[64 * e:64 * e + 64, bank, 0:I],
                                                  xgT[j][:, k, 64 * e:64 * e + 64], w[:, e, k, :],
                                                  start=(k == 0), stop=(k == HC - 1))
                mm.then_inc(s["egu_mm"], 1)

            def acts(i, j, first=False):
                pe.wait_ge(s["h_ready"], 2 * i + j + 1)
                pe.wait_ge(s["sel_ready"], 2 * i + j + 1)
                if not first:
                    pe.wait_ge(s["hT_ready"], 2 * i + j)
                flip(1, 0, [hh[j][:, 0:2 * P:2], hh[j][:, 1:2 * P:2], hh[j][:, 2 * P:3 * P]])
                nc.tensor.matmul(ps[:, 1, IC * P:IC * P + P], sel[j][:].to_broadcast([NPAIR, P]), tab[:, 0::2],
                                 start=True, stop=True).then_inc(s["hT_mm"], 1)

            def down_mm(i, j, first=False):
                pe.wait_ge(s["hT_ready"], 2 * i + j + 1)
                for n in range(4, PIECES):
                    pe.wait_ge(w_in[j][n], 16 * (i + 1))
                if not first:
                    pe.wait_ge(s["y_ready"], 2 * i + j - 1)
                for k in range(IC):
                    for e in range(2):
                        mm = nc.tensor.matmul(ps[64 * e:64 * e + 64, 6 + j, :], hT[j][:, k, 64 * e:64 * e + 64],
                                              wd[j][:, e, k, :], start=(k == 0), stop=(k == IC - 1))
                mm.then_inc(s["y_mm"], 1)

            def merge(i, j):
                pe.wait_ge(s["yw_ready"], 2 * i + j + 1)
                pe.wait_ge(s["same_ready"], 2 * i + j + 1)
                nc.tensor.matmul(ps[:, 6 + j, :], same[j], yw[j], start=True, stop=True)\
                    .then_inc(s["merged_mm"], 1)

            tokens(0, 0, True)
            tokens(0, 1)
            gate_up_mm(0, 0, True)
            acts(0, 0, True)
            tokens(1, 0)
            gate_up_mm(0, 1, True)
            down_mm(0, 0, True)
            acts(0, 1)
            merge(0, 0)

            def two_pairs(i, first=False):
                tokens(i, 1)
                gate_up_mm(i, 0)
                down_mm(i - 1, 1, first)
                acts(i, 0)
                merge(i - 1, 1)
                tokens(i + 1, 0)
                gate_up_mm(i, 1)
                down_mm(i, 0)
                acts(i, 1)
                merge(i, 0)

            two_pairs(1, True)
            with pe.Fori(2, NPAIR // 2 - 1) as i:
                two_pairs(i)
            i = NPAIR // 2 - 1
            tokens(i, 1)
            gate_up_mm(i, 0)
            down_mm(i - 1, 1)
            acts(i, 0)
            merge(i - 1, 1)
            gate_up_mm(i, 1)
            down_mm(i, 0)
            acts(i, 1)
            merge(i, 0)
            down_mm(i, 1)
            merge(i, 1)

        @block.scalar
        def _(act):
            def copy(dst, src, sm):
                nc.scalar.copy(dst, src).then_inc(sm, 1)

            act.wait_ge(s["par_in"], 16 * 9)
            nc.scalar.activation(An[:], An[:], ACT.Exp).then_inc(s["a_exp"], 1)
            act.wait_ge(s["pre_t"], 2)
            for m in range(2):
                copy(winT[:, m, :], ps[:, 4 + m, :], s["pre_ev"])
            act.wait_ge(s["pre_t"], 3)
            copy(gwT[:], ps[:, 6, 0:HC * E].rearrange("p (c e) -> p c e", c=HC), s["pre_ev"])
            act.wait_ge(s["pre_t"], 4)
            w = DR + 2 * NS
            copy(xpT[:], ps[:, 7, 0:DC * w].rearrange("p (c r) -> p c r", c=DC), s["pre_ev"])
            copy(vec[:], ps[:, 7, 256:256 + 3 * DC], s["pre_ev"])
            act.wait_ge(s["pre_t"], 5)
            copy(dtwT[:], ps[0:DR, 4, :], s["pre_ev"])

            used = {}

            for kind, b, c in mine("act"):
                p = b % 2
                if kind == "ctx":
                    for m in range(2):
                        act.wait_ge(s["ctxT_mm"], 2 * b + m + 1)
                        if b >= 1:
                            act.wait_ge(s["inproj_mm"], DC * b)
                        copy(ctxT[:, m, :], ps[:, 4 + m, :], s["ctxT_ready"])
                elif kind == "xpad":
                    if b == 0 and c == 0:
                        act.wait_ge(s["const_set"], 4)
                    act.wait_ge(s["inproj_mm"], DC * b + c + 1)
                    if b >= 1:
                        act.wait_ge(s["conv_done"], DC * (b - 1) + c + 1)
                        act.wait_ge(s["xdbl_mm"], b)
                        act.wait_ge(s["dtu_ready"], b)
                    nc.scalar.activation(u[:, c, :], ps[:, 4 + c % 2, :], ACT.Identity, bias=vec[:, c:c + 1],
                                         scale=cw[:, c, TAPS - 1:TAPS])
                    copy(xpad[:, c, TAPS - 1:XP], ps[:, 4 + c % 2, :], s["xpad_ready"])
                elif kind == "tanh":
                    if b >= 1:
                        act.wait_ge(s["dt_ready"], b)
                    act.wait_ge(s["conv_done"], DC * b + c + 1)
                    nc.scalar.activation(bt1[:, c, :], u[:, c, :], ACT.Tanh).then_inc(s["tanh_ready"], 1)
                elif kind == "xdbl":
                    act.wait_ge(s["xdbl_mm"], b + 1)
                    if b >= 1:
                        act.wait_ge(s["dt_mm"], DC * b)
                        act.wait_ge(s["bc_st"], 16 * b)
                    copy(xdbl[:], ps[0:DR + 2 * NS, 4, :], s["xdbl_ready"])
                elif kind == "xs":
                    act.wait_ge(s["dt_mm"], DC * b + c + 1)
                    nc.scalar.activation(dt[p][:, c, :], ps[:, 5 - c % 2, :], ACT.Identity,
                                         bias=vec[:, DC + c:DC + c + 1]).then_inc(s["xs_done"], 1)
                elif kind == "exp":
                    act.wait_ge(s["xm_ready"], b + 1)
                    act.wait_ge(s["u_ready"], DC * (b + 1))
                    nc.scalar.activation(bt1[:], dtu[p], ACT.Exp).then_inc(s["e_ready"], 1)
                elif kind == "ln":
                    act.wait_ge(s["ser_ready"], DC * (b + 1))
                    nc.scalar.activation(bt1[:], bt1[:], ACT.Ln, bias=1.0).then_inc(s["l_ready"], 1)
                elif kind == "du":
                    act.wait_ge(s["dt_ready"], b + 1)
                    act.wait_ge(s["u_ready"], DC * (b + 1))
                    nc.scalar.activation(bt2[:, c, :], u[:, c, :], ACT.Copy,
                                         scale=vec[:, 2 * DC + c:2 * DC + c + 1]).then_inc(s["du_ready"], 1)
                elif kind == "dA":
                    q = b * STEPS + c
                    g, k = divmod(c, DC)
                    act.wait_ge(s["dt_ready"], b + 1)
                    if q >= 2:
                        act.wait_ge(s["scan_done"], q - 1)
                    for n in range(NB):
                        a = nc.scalar.activation(dA[q % 2][:, n, 1:L], dt[p][:, k, 1:L], ACT.Exp,
                                                 scale=An[:, k, NB * g + n:NB * g + n + 1])
                    a.then_inc(s["dA_done"], 1)
                elif kind == "gate":
                    act.wait_ge(s["gsc_ready"], 2 * b + 1)
                    if c % 2 in used:
                        act.wait_ge(*used[c % 2])
                    if b >= 1:
                        act.wait_ge(s["xnT_mm"], HC * b)
                        act.wait_ge(s["xn_st"], 16 * b)
                    for dst, f in ((zx[:, c, :], ACT.Identity), (tg[c % 2][:], ACT.Tanh)):
                        a = nc.scalar.activation(dst, xb[p][:, c, :], f, bias=gsc[:, c, 1:2], scale=gsc[:, c, 0:1])
                    a.then_inc(s["gth_ready"], 1)
                    used[c % 2] = (s["zg_ready"], LT * b + c + 1)
                elif kind == "zT":
                    act.wait_ge(s["zT_mm"], LT * b + c + 1)
                    if b >= 1:
                        act.wait_ge(s["yz_done"], LT * b)
                    copy(zT[:, c, :], ps[:, 4 + c % 2, :], s["zT_ready"])
                elif kind == "xn":
                    act.wait_ge(s["gsc_ready"], 2 * b + 2)
                    act.wait_ge(s["zT_mm"], LT * (b + 1))
                    nc.scalar.activation(zx[:, c, :], xb[p][:, c, :], ACT.Identity, bias=gsc[:, c, 1:2],
                                         scale=gsc[:, c, 0:1]).then_inc(s["xn_ready"], 1)
                elif kind == "xnT":
                    act.wait_ge(s["xnT_mm"], HC * b + c + 1)
                    if b >= 1:
                        act.wait_ge(s["gu_mm"], NI * b)
                        act.wait_ge(s["lg_mm"], LT * b)
                    copy(xnT[:, c, :], ps[:, 4 + c % 2, :], s["xnT_ready"])
                elif kind == "logits":
                    n = LT * b + c
                    act.wait_ge(s["lg_mm"], n + 1)
                    if n >= 1:
                        act.wait_ge(s["slot_ready"], n)
                    copy(lg[:], ps[:, 4, 0:E], s["lg_ready"])
                elif kind == "weights":
                    n = LT * b + c
                    act.wait_ge(s["m_ready"], n + 1)
                    act.wait_ge(s["lg_ready"], n + 1)
                    nc.scalar.activation(ohp[:, 0, :], lg[:], ACT.Exp, bias=negm[:], accum_out=ssum[:])
                    nc.scalar.activation(e6[:], m8[:, 0:K], ACT.Exp, bias=negm[:]).then_inc(s["ex_ready"], 1)
                elif kind == "shared":
                    m = ISC[c]
                    act.wait_ge(s["g_mm"], NI * b + c + 1)
                    if c % 2 in used:
                        act.wait_ge(*used[c % 2])
                    nc.scalar.activation(tg[c % 2][0:m, :], ps[0:m, 6, :], ACT.Tanh, scale=0.5)\
                        .then_inc(s["sth_ready"], 1)
                    used[c % 2] = (s["hs_ready"], NI * b + c + 1)

            def evac_tokens(i, j, first=False):
                act.wait_ge(s["xgT_mm"], 2 * i + j + 1)
                if not first:
                    act.wait_ge(s["egu_mm"], 2 * i + j - 1)
                copy(xgT[j], ps[:, 0, :].rearrange("p (c t) -> p c t", c=HC), s["xgT_ready"])

            def silu(i, j, first=False):
                act.wait_ge(s["egu_mm"], 2 * i + j + 1)
                if not first:
                    act.wait_ge(s["hT_mm"], 2 * i + j - 1)
                nc.scalar.activation(hh[j][:, 0:I], ps[:, 2 + j, 0:I], ACT.Silu).then_inc(s["silu_ready"], 1)

            def evac_acts(i, j, first=False):
                act.wait_ge(s["hT_mm"], 2 * i + j + 1)
                if not first:
                    act.wait_ge(s["y_mm"], 2 * i + j - 1)
                    act.wait_ge(s["same_ready"], 2 * i + j - 1)
                copy(hT[j], ps[:, 1, :].rearrange("p (c t) -> p c t", c=IC + 1), s["hT_ready"])

            def evac_merged(i, j, first=False):
                act.wait_ge(s["merged_mm"], 2 * i + j + 1)
                if not first:
                    act.wait_ge(s["scat"], 16 * (2 * i + j - 1))
                copy(ys[j], ps[:, 6 + j, :], s["y_ready"])

            evac_tokens(0, 0, True)
            evac_tokens(0, 1, True)
            silu(0, 0, True)
            evac_acts(0, 0, True)
            evac_tokens(1, 0)
            silu(0, 1, True)
            evac_acts(0, 1, True)
            evac_merged(0, 0, True)

            def two_pairs(i, first=False):
                evac_tokens(i, 1)
                silu(i, 0)
                evac_acts(i, 0)
                evac_merged(i - 1, 1, first)
                evac_tokens(i + 1, 0)
                silu(i, 1)
                evac_acts(i, 1)
                evac_merged(i, 0)

            two_pairs(1, True)
            with act.Fori(2, NPAIR // 2 - 1) as i:
                two_pairs(i)
            i = NPAIR // 2 - 1
            evac_tokens(i, 1)
            silu(i, 0)
            evac_acts(i, 0)
            evac_merged(i - 1, 1)
            silu(i, 1)
            evac_acts(i, 1)
            evac_merged(i, 0)
            evac_merged(i, 1)

        @block.vector
        def _(dve):
            count = [0]

            def link(ins):
                count[0] += 1
                ins.then_inc(s["dve"], 1)
                dve.wait_ge(s["dve"], count[0])

            V = nc.vector

            link(V.memset(zeros, 0.0))
            link(V.memset(csum[:], 0.0))
            for a in dA:
                link(V.memset(a[:, :, 0:1], 0.0))
            link(V.memset(xpad[:, :, 0:TAPS - 1], 0.0))
            dve.wait_ge(s["par_in"], 16 * 9)
            link(V.tensor_scalar(cw[:], cw[:], 0.5, None, ALU.mult))
            dve.wait_ge(s["pre_ev"], 6)
            link(V.tensor_scalar(vec[:, 0:DC], vec[:, 0:DC], 0.5, None, ALU.mult))
            dve.wait_ge(s["a_exp"], 1)
            V.tensor_scalar(An[:], An[:], -1.0, None, ALU.mult).then_inc(s["const_set"], 1)

            def scan(q, b, c):
                dve.wait_ge(s["dA_done"], q + 1)
                dve.wait_ge(s["dbu_done"], q + 1)
                V.tensor_tensor_scan(S[q % 4].rearrange("p n l -> p (n l)"), dA[q % 2].rearrange("p n l -> p (n l)"),
                                     S[q % 4].rearrange("p n l -> p (n l)"), 0.0, ALU.mult, ALU.add)\
                    .then_inc(s["scan_done"], 1)

            def weigh(q):
                n = q // DC
                dve.wait_ge(s["scan_done"], q + 1)
                dve.wait_ge(rep_in[n % 2], 32 * (n // 2 + 1))
                V.tensor_tensor(S[q % 4], S[q % 4], Crep[n % 2], ALU.mult).then_inc(s["cs_done"], 1)

            for kind, b, c in mine("dve"):
                p = b % 2
                if kind == "conv":
                    a = u[:, c, :]
                    dve.wait_ge(s["xpad_ready"], DC * b + c + 1)
                    for k in range(TAPS - 1):
                        ins = V.scalar_tensor_tensor(a, xpad[:, c, k:k + L], cw[:, c, k:k + 1], a,
                                                     ALU.mult, ALU.add)
                        if k < TAPS - 2:
                            link(ins)
                    ins.then_inc(s["conv_done"], 1)
                elif kind == "u":
                    dve.wait_ge(s["tanh_ready"], DC * b + c + 1)
                    V.scalar_tensor_tensor(u[:, c, :], bt1[:, c, :], 1.0, u[:, c, :], ALU.add, ALU.mult)\
                        .then_inc(s["u_ready"], 1)
                elif kind == "xm":
                    dve.wait_ge(s["xs_done"], DC * (b + 1))
                    if b >= 2:
                        dve.wait_ge(s["dbu_done"], STEPS * (b - 1))
                    V.tensor_scalar(dtu[p], dt[p], 40.0, None, ALU.min).then_inc(s["xm_ready"], 1)
                elif kind == "softplus":
                    dve.wait_ge(s["l_ready"], b + 1)
                    link(V.copy_predicated(bt1[:], bt2[:].bitcast(U32), dtu[p]))
                    V.tensor_tensor(dt[p], dt[p], bt1[:], ALU.max).then_inc(s["dt_ready"], 1)
                    dve.wait_ge(s["dt_ready"], b + 1)
                    V.tensor_tensor(dtu[p], dt[p], u, ALU.mult).then_inc(s["dtu_ready"], 1)
                elif kind == "scan":
                    scan(b * STEPS + c, b, c)
                elif kind == "weigh":
                    weigh(b * STEPS + c)
                elif kind in ("gate_stats", "x2"):
                    if kind == "gate_stats":
                        dve.wait_ge(x_in[p], 16 * (b // 2 + 1))
                    else:
                        dve.wait_ge(s["yz_done"], LT * b + c + 1)
                        link(V.tensor_tensor(xb[p][:, c, :], xb[p][:, c, :], zT[:, c, :], ALU.add))
                    link(V.bn_stats(stats[:, c, :], xb[p][:, c, :]))
                    link(V.bn_aggr(mv[:, c, :], stats[:, c, :]))
                elif kind in ("gate_var", "var"):
                    if kind == "var":
                        dve.wait_ge(s["zg_ready"], LT * (b + 1))
                    V.tensor_scalar(gsc[:, :, 0], mv[:, :, 1], EPS, None, ALU.add).then_inc(s["var_ready"], 1)
                elif kind in ("gate_scale", "scale"):
                    dve.wait_ge(s["rstd_ready"], 2 * b + 1 + (kind == "scale"))
                    if kind == "gate_scale":
                        link(V.tensor_scalar(gsc[:, :, 0], gsc[:, :, 0], 0.5, None, ALU.mult))
                    V.scalar_tensor_tensor(gsc[:, :, 1], mv[:, :, 0], -1.0, gsc[:, :, 0], ALU.mult, ALU.mult)\
                        .then_inc(s["gsc_ready"], 1)
                elif kind == "gate":
                    dve.wait_ge(s["gth_ready"], LT * b + c + 1)
                    V.scalar_tensor_tensor(zx[:, c, :], tg[c % 2][:], 1.0, zx[:, c, :], ALU.add, ALU.mult)\
                        .then_inc(s["zg_ready"], 1)
                elif kind == "yz":
                    dve.wait_ge(s["yT_done"], STEPS * (b + 1))
                    dve.wait_ge(s["zT_ready"], LT * (b + 1))
                    for t in range(LT):
                        V.tensor_tensor(zT[:, t, :], ps_y[:, t, :], zT[:, t, :], ALU.mult).then_inc(s["yz_done"], 1)
                elif kind == "choose":
                    n = LT * b + c
                    if n == 0:
                        dve.wait_ge(s["iota_set"], 1)
                    dve.wait_ge(s["lg_ready"], n + 1)
                    link(V.max(m8[:], lg[:]))
                    V.tensor_scalar(negm[:], m8[:, 0:1], -1.0, None, ALU.mult).then_inc(s["m_ready"], 1)
                    link(V.max_index(i8[:], m8[:], lg[:]))
                    link(V.tensor_copy(i8f[:], i8[:, 0:K]))
                    link(V.tensor_tensor(oh[:], iota_e[:, None, :].to_broadcast([P, K, E]),
                                         i8f[:, :, None].to_broadcast([P, K, E]), ALU.is_equal))
                    if n >= 1:
                        dve.wait_ge(s["pos_mm"], n)
                        link(V.tensor_tensor(csum[:], csum[:], mask[:], ALU.add))
                    with nc.allow_low_precision("sums of one-hot rows, exact"):
                        V.tensor_reduce(mask[:], oh[:].rearrange("p k e -> p e k"), AX_X, ALU.add)\
                            .then_inc(s["mask_ready"], 1)
                elif kind == "slots":
                    n = LT * b + c
                    dve.wait_ge(s["ex_ready"], n + 1)
                    link(V.reciprocal(ssum[:], ssum[:]))
                    link(V.tensor_scalar(rec[:, n, :, 1], e6[:], ssum[:], None, ALU.mult))
                    V.tensor_copy(rec[:, n, :, 0], tokid[:, n:n + 1].to_broadcast([P, K]))
                    dve.wait_ge(s["pos_mm"], n + 1)
                    link(V.tensor_tensor(ohp[:], oh[:], ps[:, 5, None, 0:E].to_broadcast([P, K, E]), ALU.mult))
                    link(V.tensor_reduce(posk[:], ohp[:], AX_X, ALU.add))
                    link(V.scalar_tensor_tensor(slotf[:], i8f[:], float(CAP), posk[:], ALU.mult, ALU.add))
                    link(V.tensor_scalar(over[:], posk[:], float(CAP), float(2 * E * CAP), ALU.is_ge, ALU.mult))
                    V.tensor_tensor(slotu[:, n, :], slotf[:], over[:], ALU.add).then_inc(s["slot_ready"], 1)
                elif kind == "shared":
                    m = ISC[c]
                    th = tg[c % 2][0:m, :]
                    dve.wait_ge(s["sth_ready"], NI * b + c + 1)
                    if b >= 1:
                        dve.wait_ge(s["dn_mm"], LT * b)
                    link(V.scalar_tensor_tensor(th, th, 1.0, ps[0:m, 6, :], ALU.add, ALU.mult))
                    dve.wait_ge(s["gu_mm"], NI * b + c + 1)
                    V.scalar_tensor_tensor(hs[0:m, c, :], th, 0.5, ps[0:m, 7, :], ALU.mult, ALU.mult)\
                        .then_inc(s["hs_ready"], 1)
                elif kind == "down":
                    dve.wait_ge(s["dn_mm"], LT * b + c + 1)
                    V.tensor_tensor(xb[p][:, c, :], xb[p][:, c, :], ps[:, 6 + c % 2, :], ALU.add)\
                        .then_inc(s["ob_ready"], 1)
                elif kind == "pads":
                    dve.wait_ge(s["yT_done"], B * STEPS)
                    for j in range(2):
                        V.memset(wd[j][96:P, :, 2, :], 0.0).then_inc(s["pad_set"], 1)
                        V.memset(hh[j][:, I:IC * P], 0.0)

            dve.wait_ge(s["tab_mm"], 1)
            V.tensor_copy(ids, ps[:, 4, 0:NPAIR]).then_inc(s["ids_ready"], 1)
            V.tensor_copy(meta[:, :, 0], ps[:, 4, 0:NPAIR]).then_inc(s["ids_ready"], 1)
            V.tensor_copy(meta[:, :, 2], ps[:, 4, 64:64 + NPAIR]).then_inc(s["ids_ready"], 1)
            dve.wait_ge(s["ids_ready"], 3)
            link(V.tensor_scalar(is_odd[:], spare[:], float(TRASH + CAP), None, ALU.is_ge))
            link(V.tensor_scalar(meta[:, :, 1], meta[:, :, 0], -1.0, spare[:], ALU.mult, ALU.add))
            link(V.tensor_scalar(meta[:, :, 1], meta[:, :, 1], is_odd[:], None, ALU.mult))

            def at_pair(t, i, j):
                return t[:, 2 * i + j] if isinstance(i, int) else t[:, bass.ds(2 * i + j, 1)]

            def index(i, j, first=False):
                if not first:
                    dve.wait_ge(s["xgT_mm"], 2 * i + j - 1)
                src = ids[:, 2 * i + j:2 * i + j + 1] if isinstance(i, int) else ids[:, bass.ds(2 * i + j, 1)]
                V.tensor_copy(idxg[j][:], src).then_inc(s["idx_ready"], 1)

            def select(i, j, first=False):
                q = 2 * i + j
                if not first:
                    dve.wait_ge(s["hT_mm"], q - 1)
                src = ident[0:NPAIR, q:q + 1] if isinstance(i, int) else ident[0:NPAIR, bass.ds(q, 1)]
                V.tensor_copy(sel[j][:], src).then_inc(s["sel_ready"], 1)

            def gated(i, j, first=False):
                select(i, j, first)
                dve.wait_ge(s["silu_ready"], 2 * i + j + 1)
                V.tensor_tensor(hh[j][:, 0:I], hh[j][:, 0:I], ps[:, 4 + j, 0:I], ALU.mult).then_inc(s["h_ready"], 1)

            def match(i, j, first=False):
                q = 2 * i + j
                col = mcol[j][:] if isinstance(i, int) else mcol[j][:, None, :]
                V.tensor_copy(col, at_pair(meta, i, j)).then_inc(s["w_ready"], 1)
                dve.wait_ge(s["w_ready"], q + 1)
                dve.wait_ge(s["hT_ready"], q + 1)
                if not first:
                    dve.wait_ge(s["merged_mm"], q - 1)
                V.tensor_scalar(same[j], hT[j][:, IC, :], mcol[j][:, 0:1], None, ALU.is_equal)\
                    .then_inc(s["same_ready"], 1)
                dve.wait_ge(s["same_ready"], q + 1)
                V.tensor_reduce(dup[:], same[j][:, 0:CAP], AX_X, ALU.add).then_inc(s["dup_ready"], 1)
                dve.wait_ge(s["dup_ready"], q + 1)
                if not first:
                    dve.wait_ge(s["scat"], 16 * (q - 1))
                V.scalar_tensor_tensor(idxs[j][:], dup[:], mcol[j][:, 1:2], mcol[j][:, 0:1], ALU.mult, ALU.add)\
                    .then_inc(s["idxs_ready"], 1)

            def weighted(i, j, first=False):
                dve.wait_ge(s["y_mm"], 2 * i + j + 1)
                if not first:
                    dve.wait_ge(s["merged_mm"], 2 * i + j - 1)
                V.tensor_scalar(yw[j], ps[:, 6 + j, :], mcol[j][:, 2:3], None, ALU.mult).then_inc(s["yw_ready"], 1)

            index(0, 0, True)
            index(0, 1, True)
            index(1, 0)
            index(1, 1)
            gated(0, 0, True)
            match(0, 0, True)
            index(2, 0)
            gated(0, 1, True)
            weighted(0, 0, True)
            match(0, 1, True)

            def two_pairs(i, first=False, more=True):
                index(i + 1, 1)
                gated(i, 0)
                weighted(i - 1, 1, first)
                match(i, 0)
                if more:
                    index(i + 2, 0)
                gated(i, 1)
                weighted(i, 0)
                match(i, 1)

            two_pairs(1, True)
            with dve.Fori(2, NPAIR // 2 - 2) as i:
                two_pairs(i)
            two_pairs(NPAIR // 2 - 2, more=False)
            i = NPAIR // 2 - 1
            gated(i, 0)
            weighted(i - 1, 1)
            match(i, 0)
            gated(i, 1)
            weighted(i, 0)
            match(i, 1)
            weighted(i, 1)

        @block.gpsimd
        def _(pool):
            G = nc.gpsimd
            G.iota(initrow[:, :, 0], pattern=[[1, P]], base=TRASH, channel_multiplier=0,
                   allow_small_or_imprecise_dtypes=True)
            G.memset(initrow[:, :, 1], 0.0)
            pool.wait_ge(s["dve"], 1)
            G.memset(ones[:], 1.0).then_inc(s["const_set"], 1)
            G.memset(ident[:], 0.0)
            G.memset(ltri[:], 1.0).then_inc(s["ser_chain"], 1)
            pool.wait_ge(s["ser_chain"], 1)
            G.affine_select(out=ident[:], in_=ident[:], compare_op=ALU.not_equal, fill=1.0, base=0,
                            pattern=[[-1, P]], channel_multiplier=1).then_inc(s["const_set"], 1)
            G.affine_select(out=ltri[:], in_=ltri[:], compare_op=ALU.is_gt, fill=0.0, base=0,
                            pattern=[[1, P]], channel_multiplier=-1).then_inc(s["const_set"], 1)
            G.memset(mhalf[:], -0.5)
            G.iota(spare[:], pattern=[[1, 1]], base=TRASH, channel_multiplier=1, allow_small_or_imprecise_dtypes=True)
            G.iota(iota_e[:], pattern=[[1, E]], base=0, channel_multiplier=0, allow_small_or_imprecise_dtypes=True)
            G.iota(tokid[:], pattern=[[P, B * LT]], base=0, channel_multiplier=1,
                   allow_small_or_imprecise_dtypes=True).then_inc(s["iota_set"], 1)
            chain = [1]

            def link(ins):
                chain[0] += 1
                ins.then_inc(s["ser_chain"], 1)
                pool.wait_ge(s["ser_chain"], chain[0])

            for kind, b, c in mine("pool"):
                p = b % 2
                if kind in ("gate_rstd", "rstd"):
                    pool.wait_ge(s["var_ready"], 2 * b + 1 + (kind == "rstd"))
                    G.tensor_tensor(gsc[:, :, 0], gsc[:, :, 0], mhalf[:], ALU.pow).then_inc(s["rstd_ready"], 1)
                elif kind == "series":
                    pool.wait_ge(s["e_ready"], b + 1)
                    if b == 0:
                        pool.wait_ge(s["init_in"], 16 * 3)
                    else:
                        pool.wait_ge(s["duT_done"], b)
                    e, low, sr = bt1[:, c, :], bt2[:, c, :], dtu[p][:, c, :]
                    link(G.tensor_scalar(low, e, SERIES_BELOW, None, ALU.min))
                    link(G.tensor_scalar(sr, low, -0.25, 1.0 / 3.0, ALU.mult, ALU.add))
                    link(G.tensor_tensor(sr, sr, low, ALU.mult))
                    link(G.tensor_scalar(sr, sr, -0.5, None, ALU.add))
                    link(G.tensor_tensor(sr, sr, low, ALU.mult))
                    link(G.tensor_scalar(sr, sr, 1.0, None, ALU.add))
                    link(G.tensor_tensor(sr, sr, low, ALU.mult))
                    G.tensor_scalar(low, e, SERIES_BELOW, None, ALU.is_lt).then_inc(s["ser_ready"], 1)
                elif kind == "dbu":
                    q = b * STEPS + c
                    n, k = divmod(q, DC)
                    pool.wait_ge(s["dtu_ready"], b + 1)
                    pool.wait_ge(rep_in[n % 2], 32 * (n // 2 + 1))
                    if q >= 4:
                        pool.wait_ge(s["yT_done"], q - 3)
                    G.tensor_tensor(S[q % 4], dtu[p][:, k, None, :].to_broadcast([P, NB, L]), Brep[n % 2], ALU.mult)\
                        .then_inc(s["dbu_done"], 1)
                elif kind == "scatter":
                    n = LT * b + c
                    pool.wait_ge(s["slot_ready"], n + 1)
                    for k in range(K):
                        G.indirect_dma_start(
                            out=slot_dram, out_offset=bass.IndirectOffsetOnAxis(ap=slotu[:, n, k:k + 1], axis=0),
                            in_=rec[:, n, k, :], in_offset=None, bounds_check=E * CAP - 1, oob_is_err=False)\
                            .then_inc(s["scattered"], 16)

            pool.wait_ge(s["xn_st"], 16 * B)
            pool.wait_ge(s["out_st"], 16 * B)

            def hold():
                pool.sem_inc(s["held"], 1)

            def gather(i, j, first=False):
                pool.wait_ge(s["idx_ready"], 2 * i + j + 1)
                if not first:
                    pool.wait_ge(s["xgT_mm"], 2 * i + j - 1)
                hold()
                G.indirect_dma_start(out=xg[j], out_offset=None, in_=xn_dram,
                                     in_offset=bass.IndirectOffsetOnAxis(ap=idxg[j][:], axis=0),
                                     bounds_check=T + P - 1, oob_is_err=True).then_inc(xg_in[j], 16)

            def scatter(i, j, first=False):
                pool.wait_ge(s["y_ready"], 2 * i + j + 1)
                pool.wait_ge(s["idxs_ready"], 2 * i + j + 1)
                if not first:
                    pool.wait_ge(s["scat"], 16 * (2 * i + j))
                hold()
                G.indirect_dma_start(out=out, out_offset=bass.IndirectOffsetOnAxis(ap=idxs[j][:], axis=0),
                                     in_=ys[j], in_offset=None, bounds_check=T + P - 1, oob_is_err=True,
                                     compute_op=ALU.add).then_inc(s["scat"], 16)

            gather(0, 0, True)
            gather(0, 1, True)
            gather(1, 0)
            gather(1, 1)
            scatter(0, 0, True)
            gather(2, 0)
            scatter(0, 1)
            with pool.Fori(1, NPAIR // 2 - 2) as i:
                gather(i + 1, 1)
                scatter(i, 0)
                gather(i + 2, 0)
                scatter(i, 1)
            gather(NPAIR // 2 - 1, 1)
            for j in range(2):
                scatter(NPAIR // 2 - 2, j)
            for j in range(2):
                scatter(NPAIR // 2 - 1, j)


_INS = ['x', 'ctx_1024', 'L0_xattn_in_proj_w', 'L0_xattn_conv_w', 'L0_xattn_conv_b', 'L0_xattn_x_proj_w',
        'L0_xattn_dt_proj_w', 'L0_xattn_dt_proj_b', 'L0_xattn_A_log', 'L0_xattn_D', 'L0_ffn_gate_w',
        'L0_ffn_w_gate', 'L0_ffn_w_up', 'L0_ffn_w_down', 'L0_ffn_sw_gate', 'L0_ffn_sw_up', 'L0_ffn_sw_down']


def kernel(**inputs):
    import numpy as np
    import concourse.bacc as bacc
    from concourse.bass_utils import run_bass_kernel_spmd

    nc = bacc.Bacc("TRN2", target_bir_lowering=False, num_devices=1, dynamic_dma_scratch_size=4096)
    arrays, args = {}, []
    for name in _INS:
        a = np.ascontiguousarray(inputs[name])
        arrays[f"in_{name}"] = a
        args.append(nc.dram_tensor(f"in_{name}", a.shape, mybir.dt.from_np(a.dtype), kind="ExternalInput").ap())
    out = nc.dram_tensor("out_rows", [T + P, H], F32, kind="ExternalOutput").ap()
    build(nc, *args, out)
    r = run_bass_kernel_spmd(nc, [arrays], core_ids=[0])
    return r.results[0]["out_rows"][:T].reshape(B, L, H)
```
